# Optimizing a Trainium2 kernel written in Bass

```python
import numpy as np
import jax
import jax.numpy as jnp

def _softmax(x, axis=-1):
    return jax.nn.softmax(x, axis=axis)

def _gelu(x):
    return jax.nn.gelu(x, approximate=True)

def _silu(x):
    return jax.nn.silu(x)

def _sigmoid(x):
    return jax.nn.sigmoid(x)

def _layernorm(x, axis=-1, eps=1e-05):
    m = jnp.mean(x, axis=axis, keepdims=True)
    v = jnp.var(x, axis=axis, keepdims=True)
    return (x - m) / jnp.sqrt(v + eps)

def _scatter_add(tgt, idx, src, axis=0):
    return tgt.at[idx].add(src)

def _segment_sum(src, seg, n):
    return jax.ops.segment_sum(src, seg, n)
kernel_name = 'mk_prb_d1_jaxref_r8_1775c2'

def setup_inputs(seed: int=0):
    np.random.seed(seed)
    _w = jnp.asarray

    def _L0_attn_setup():
        import jax, jax.numpy as jnp
        import numpy as np
        NUM_HEADS = 8
        NORM_EPS = 1e-05

        def _gla_scan(q, k, v, g):
            B, T, H, Dk = q.shape
            Dv = v.shape[-1]
            qs, ks, vs, gs = [jnp.swapaxes(x, 0, 1) for x in (q, k, v, g)]

            def step(S, inp):
                qt, kt, vt, gt = inp
                S = jnp.exp(gt)[..., None] * S + kt[..., None] * vt[..., None, :]
                ot = jnp.einsum('bhk,bhkv->bhv', qt, S)
                return (S, ot)
            S0 = jnp.zeros((B, H, Dk, Dv), jnp.float32)
            _, o = jax.lax.scan(step, S0, (qs, ks, vs, gs))
            return jnp.swapaxes(o, 0, 1)
        key = jax.random.key(seed)
        ks = jax.random.split(key, 5)
        B, T, D = (4, 256, 128)
        s = 0.02
        return {'hidden_states': jax.random.normal(ks[0], (B, T, D), jnp.float32), 'Wq': jax.random.normal(ks[1], (D, D), jnp.float32) * s, 'Wf': jax.random.normal(ks[2], (D, D), jnp.float32) * s, 'Wi': jax.random.normal(ks[3], (D, D), jnp.float32) * s, 'g_weight': jnp.ones((D,), jnp.float32), 'Wo': jax.random.normal(ks[4], (D, D), jnp.float32) * s}
    _L0_attn_in = _L0_attn_setup()

    def _L0_ffn_setup():
        import jax, jax.numpy as jnp
        import numpy as np
        import math
        MAX_NORM = 0.95
        CURVATURE = 1.0
        TOP_K = 2
        EPS = 1e-07

        def _project_to_ball(x):
            norm = jnp.clip(jnp.linalg.norm(x, axis=-1, keepdims=True), EPS, None)
            scale = jnp.where(norm > MAX_NORM, MAX_NORM / norm, jnp.ones_like(norm))
            return x * scale
        key = jax.random.key(seed)
        ks = jax.random.split(key, 8)
        B, N, D, E, F = (2, 256, 128, 8, 512)
        x = jax.random.normal(ks[0], (B, N, D), dtype=jnp.float32)
        c = jax.random.normal(ks[1], (E, D), dtype=jnp.float32)
        centroids = c / jnp.linalg.norm(c, axis=-1, keepdims=True) * 0.5
        Wp = jax.random.normal(ks[2], (D, D), dtype=jnp.float32) * 0.02
        bp = jnp.zeros((D,), dtype=jnp.float32)
        W1 = jax.random.normal(ks[3], (E, D, F), dtype=jnp.float32) * 0.02
        b1 = jnp.zeros((E, F), dtype=jnp.float32)
        W2 = jax.random.normal(ks[4], (E, F, D), dtype=jnp.float32) * 0.02
        b2 = jnp.zeros((E, D), dtype=jnp.float32)
        return {'x': x, 'centroids': centroids, 'Wp': Wp, 'bp': bp, 'W1': W1, 'b1': b1, 'W2': W2, 'b2': b2}
    _L0_ffn_in = _L0_ffn_setup()
    _d = {'L0_attn_hidden_states': _L0_attn_in['hidden_states'], 'L0_attn_Wq': _L0_attn_in['Wq'], 'L0_attn_Wf': _L0_attn_in['Wf'], 'L0_attn_Wi': _L0_attn_in['Wi'], 'L0_attn_g_weight': _L0_attn_in['g_weight'], 'L0_attn_Wo': _L0_attn_in['Wo'], 'L0_ffn_centroids': _L0_ffn_in['centroids'], 'L0_ffn_Wp': _L0_ffn_in['Wp'], 'L0_ffn_bp': _L0_ffn_in['bp'], 'L0_ffn_W1': _L0_ffn_in['W1'], 'L0_ffn_b1': _L0_ffn_in['b1'], 'L0_ffn_W2': _L0_ffn_in['W2'], 'L0_ffn_b2': _L0_ffn_in['b2']}
    _x0 = _d['L0_attn_hidden_states']
    _d['L0_attn_hidden_states'] = jax.random.normal(jax.random.fold_in(jax.random.key(seed), 1), (8, 256, 128), dtype=_x0.dtype)
    del _x0
    return _d

def reference(L0_attn_hidden_states, L0_attn_Wq, L0_attn_Wf, L0_attn_Wi, L0_attn_g_weight, L0_attn_Wo, L0_ffn_centroids, L0_ffn_Wp, L0_ffn_bp, L0_ffn_W1, L0_ffn_b1, L0_ffn_W2, L0_ffn_b2):

    def _L0_attn_ref(hidden_states, Wq, Wf, Wi, g_weight, Wo):
        import jax, jax.numpy as jnp
        import numpy as np
        NUM_HEADS = 8
        NORM_EPS = 1e-05

        def _gla_scan(q, k, v, g):
            B, T, H, Dk = q.shape
            Dv = v.shape[-1]
            qs, ks, vs, gs = [jnp.swapaxes(x, 0, 1) for x in (q, k, v, g)]

            def step(S, inp):
                qt, kt, vt, gt = inp
                S = jnp.exp(gt)[..., None] * S + kt[..., None] * vt[..., None, :]
                ot = jnp.einsum('bhk,bhkv->bhv', qt, S)
                return (S, ot)
            S0 = jnp.zeros((B, H, Dk, Dv), jnp.float32)
            _, o = jax.lax.scan(step, S0, (qs, ks, vs, gs))
            return jnp.swapaxes(o, 0, 1)
        B, T, D = hidden_states.shape
        H = NUM_HEADS
        q = hidden_states @ Wq
        f = (hidden_states @ Wf).astype(jnp.float32)
        i = hidden_states @ Wi
        q = q * jax.nn.sigmoid(q)
        k = 1.0 - jax.nn.sigmoid(f)
        g = jax.nn.log_sigmoid(f)
        split = lambda x: x.reshape(B, T, H, -1)
        q, k, v, g = (split(q), split(k), split(i), split(g))
        scale = q.shape[-1] ** (-0.5)
        o = _gla_scan(q * scale, k, v, g)
        o = o.reshape(B, T, D)
        o = o * jax.lax.rsqrt(jnp.mean(o * o, axis=-1, keepdims=True) + NORM_EPS)
        o = o * g_weight
        return o @ Wo

    def _L0_ffn_ref(x, centroids, Wp, bp, W1, b1, W2, b2):
        import jax, jax.numpy as jnp
        import numpy as np
        import math
        MAX_NORM = 0.95
        CURVATURE = 1.0
        TOP_K = 2
        EPS = 1e-07

        def _project_to_ball(x):
            norm = jnp.clip(jnp.linalg.norm(x, axis=-1, keepdims=True), EPS, None)
            scale = jnp.where(norm > MAX_NORM, MAX_NORM / norm, jnp.ones_like(norm))
            return x * scale
        B, N, D = x.shape
        E = centroids.shape[0]
        x_hyper = _project_to_ball(x @ Wp + bp)
        c_proj = _project_to_ball(centroids)
        x_norm_sq = jnp.sum(x_hyper * x_hyper, axis=-1)
        c_norm_sq = jnp.sum(c_proj * c_proj, axis=-1)
        x_norm_sq = jnp.clip(x_norm_sq, None, 0.99)
        c_norm_sq = jnp.clip(c_norm_sq, None, 0.99)
        dot = jnp.einsum('bnd,ed->bne', x_hyper, c_proj)
        diff_sq = jnp.maximum(x_norm_sq[..., None] + c_norm_sq - 2.0 * dot, 0.0)
        denom = (1.0 - x_norm_sq)[..., None] * (1.0 - c_norm_sq) + EPS
        arg = jnp.clip(1.0 + 2.0 * diff_sq / denom, 1.0 + EPS, None)
        dist = jnp.arccosh(arg)
        routing_logits = -dist / math.sqrt(CURVATURE)
        top_v, top_i = jax.lax.top_k(routing_logits, TOP_K)
        top_w = jax.nn.softmax(top_v, axis=-1)
        comb = jnp.sum(jax.nn.one_hot(top_i, E, dtype=x.dtype) * top_w[..., None], axis=2)
        h = jax.nn.gelu(jnp.einsum('bnd,edf->bnef', x, W1) + b1, approximate=False)
        y = jnp.einsum('bnef,efd->bned', h, W2) + b2
        out = jnp.einsum('bne,bned->bnd', comb, y)
        return out
    x = L0_attn_hidden_states
    xn = _layernorm(x, axis=-1)
    x = x + _L0_attn_ref(xn, L0_attn_Wq, L0_attn_Wf, L0_attn_Wi, L0_attn_g_weight, L0_attn_Wo) + _L0_ffn_ref(xn, L0_ffn_centroids, L0_ffn_Wp, L0_ffn_bp, L0_ffn_W1, L0_ffn_b1, L0_ffn_W2, L0_ffn_b2)
    return x

_drawn_inputs = setup_inputs


def setup_inputs(seed=0):
    import zlib

    import numpy as np

    out = dict(_drawn_inputs(seed))
    spreads = {'L0_attn_g_weight': (1.0, 0.2),
     'L0_ffn_bp': (0.0, 0.1),
     'L0_ffn_b1': (0.0, 0.459),
     'L0_ffn_b2': (0.0, 0.1)}
    factors = {}
    for name, (base, spread) in spreads.items():
        noise = np.random.default_rng([zlib.crc32(name.encode()), seed]).standard_normal(out[name].shape)
        drawn = base * np.exp(spread * noise) if base else spread * noise
        out[name] = jnp.asarray(drawn.astype(out[name].dtype))
    for name, factor in factors.items():
        out[name] = (out[name] * factor).astype(out[name].dtype)
    return out
```

```python
from contextlib import ExitStack

import numpy as np
import concourse.bass as bass
from concourse import mybir

F32 = mybir.dt.float32
F32R = mybir.dt.float32r
I32 = mybir.dt.int32
U32 = mybir.dt.uint32
ALU = mybir.AluOpType
ACT = mybir.ActivationFunctionType
AX = mybir.AxisListType

P = 128


def gla_and_routed_experts(
    nc: bass.Bass,
    x_in: bass.AP,
    wq_in: bass.AP,
    wf_in: bass.AP,
    wi_in: bass.AP,
    gw_in: bass.AP,
    wo_in: bass.AP,
    cent_in: bass.AP,
    wp_in: bass.AP,
    bp_in: bass.AP,
    w1_in: bass.AP,
    b1_in: bass.AP,
    w2_in: bass.AP,
    b2_in: bass.AP,
    out: bass.AP,
):
    BATCH, T, D = x_in.shape
    H = 8
    DK = D // H
    E, _, F = w1_in.shape
    N = BATCH * T
    NB = N // P
    GB = 2
    G = BATCH // GB
    GT = GB * T
    BPG = GT // P
    TOPK = 2
    TILES = (N * TOPK + E * (P - 1)) // P
    FC = F // P
    TP = T + 2
    LN_EPS = RMS_EPS = 1e-5
    MAX_NORM, BALL_EPS, NORM_CAP = 0.95, 1e-7, 0.99
    ARG_MIN = float(np.float32(1.0) + np.float32(BALL_EPS))
    FAR = 1e30
    RSQRT_GUESS = float(0x5F3759DF)
    NEWTON = 3
    RMS_STEPS = 3 + 3 * NEWTON
    QSCALE = float(DK) ** -0.5
    assert D == P and GT == 512 and F == 512 and TILES == 39 and DK * H == D

    xs_dram = nc.dram_tensor("rows_by_expert", (TILES * P, D), F32).ap()
    ys_dram = nc.dram_tensor("expert_rows_out", (TILES * P, D), F32).ap()

    with ExitStack() as ctx:
        def sb(name, shape, dt=F32):
            return ctx.enter_context(nc.sbuf_tensor(name, shape, dt))

        def sem(name):
            return ctx.enter_context(nc.semaphore(name))

        bank = [ctx.enter_context(nc.psum_tensor(f"bank{i}", [P, 512], F32)) for i in range(8)]

        x_sb = sb("x_sb", [P, NB, D])
        xn = sb("xn", [P, NB, D])
        xn_t = sb("xn_t", [P, G, GT])
        acc = x_sb
        stats = sb("stats", [P, NB, 6])
        mean_var = sb("mean_var", [P, NB, 2])
        var = sb("var", [P, NB])
        rstd = sb("rstd", [P, NB])
        halves = sb("halves", [P, NB])

        wq = sb("wq", [P, D])
        wf = sb("wf", [P, D])
        wi = sb("wi", [P, D])
        wp = sb("wp", [P, D])
        wo = sb("wo", [P, D])
        gwo = sb("gwo", [P, D])
        gw = sb("gw", [P, 1])
        bp = sb("bp", [P, 1])
        w1 = sb("w1", [P, E, F])
        w2 = sb("w2", [P, E, FC * D])
        b1 = sb("b1", [P, E, F])
        b2 = sb("b2", [P, E, D])

        ident = sb("ident", [P, P])
        ones = sb("ones", [P, P])
        before = sb("before", [P, P])
        head_ones = sb("head_ones", [P, D])
        spread = sb("spread", [P, DK, D], F32R)
        gather = sb("gather", [P, DK, D])
        zeros = sb("zeros", [P, D])
        iota_e = sb("iota_e", [P, E])
        iota_e8 = sb("iota_e8", [P, E])
        tile_row = sb("tile_row", [1, TILES])
        not_first = sb("not_first", [P, E, NB])

        q_t = sb("q_t", [P, G, GT])
        gate = sb("gate", [P, BATCH, TP])
        v_t = sb("v_t", [P, BATCH, TP + 1])
        dv_f = sb("dv_f", [P, 2, GB, TP])
        dv_hi = sb("dv_hi", [P, BATCH, TP], F32R)
        dv_lo = sb("dv_lo", [P, BATCH, TP], F32R)
        sig_q = sb("sig_q", [P, 2, GT])
        state = sb("state", [P, 3, GB, TP])
        qstate = sb("qstate", [P, 2, GT])
        q_v = sb("q_v", [P, GT])
        o_t = sb("o_t", [P, GT])
        o_sq = sb("o_sq", [P, GT])
        rms = sb("rms", [P, 3, BPG])

        xp_t = sb("xp_t", [P, 2, GT])
        xp_sq = sb("xp_sq", [P, 2, GT])
        cent = sb("cent", [E, D])
        cent_sq = sb("cent_sq", [E, D])
        cent_p = sb("cent_p", [E, D])
        cent_s = sb("cent_s", [E, 4])
        cp_t = sb("cp_t", [P, E])
        cp_sq = sb("cp_sq", [P, E])
        c_n2 = sb("c_n2", [P, E])
        c_om = sb("c_om", [P, E])
        r_tok = [sb(f"r_tok{i}", [P, NB]) for i in range(8)]
        r_big = [sb(f"r_big{i}", [P, NB, E]) for i in range(10)]
        m12 = sb("m12", [P, TOPK, NB])
        u_a = sb("u_a", [P, TOPK, NB])
        u_b = sb("u_b", [P, TOPK, NB])
        u_c = sb("u_c", [P, TOPK, NB])
        weight = sb("weight", [P, TOPK, NB])
        tot = sb("tot", [P, E, NB])
        inc = sb("inc", [P, E, NB])
        exc = sb("exc", [P, E, NB])
        cnt_i = sb("cnt_i", [P, 2, E], I32)
        pad_f = sb("pad_f", [P, 3, E])
        pos_f = sb("pos_f", [P, TOPK, NB])
        pos = sb("pos", [P, TOPK, NB], U32)
        own_f = sb("own_f", [1, TILES, E])
        own_s = sb("own_s", [1, 2, TILES])
        own = sb("own", [1, TILES + 1], I32)

        xs = [sb(f"xs{i}", [P, D]) for i in range(2)]
        xs_t = [sb(f"xs_t{i}", [P, P]) for i in range(2)]
        hb = [xn_t[:, i, :] for i in range(2)]
        hg = [xn_t[:, 2 + i, :] for i in range(2)]
        h_t = [sb(f"h_t{i}", [P, F]) for i in range(2)]
        yb = [sb(f"yb{i}", [P, D]) for i in range(2)]
        y_rows = sb("y_rows", [P, TOPK, NB, D])
        spread_f = y_rows[:, 0, :, :]

        s_x = [sem(f"s_x{g}") for g in range(G)]
        s_wproj = sem("s_wproj")
        s_wexp = sem("s_wexp")
        s_wo = sem("s_wo")
        s_cent = sem("s_cent")
        s_const = sem("s_const")
        s_zero = sem("s_zero")
        s_zfill = sem("s_zfill")
        s_dve = sem("s_dve")
        s_xn = sem("s_xn")
        s_xtp = sem("s_xtp")
        s_xnt = sem("s_xnt")
        s_pp = sem("s_pp")
        s_fp = sem("s_fp")
        s_ip = sem("s_ip")
        s_qp = sem("s_qp")
        s_xp = sem("s_xp")
        s_rp = sem("s_rp")
        s_gate = sem("s_gate")
        s_v = sem("s_v")
        s_sigq = sem("s_sigq")
        s_q = sem("s_q")
        s_dvf = sem("s_dvf")
        s_dvh = sem("s_dvh")
        s_dvl = sem("s_dvl")
        s_spread = sem("s_spread")
        s_gwo = sem("s_gwo")
        s_cp = sem("s_cp")
        s_cpt = sem("s_cpt")
        s_cpe = sem("s_cpe")
        s_route = sem("s_route")
        s_rank = sem("s_rank")
        s_pos = sem("s_pos")
        s_own = sem("s_own")
        s_sent = sem("s_sent")
        s_vb = sem("s_vb")
        s_scan = sem("s_scan")
        s_qs = sem("s_qs")
        s_red = sem("s_red")
        s_qsum = sem("s_qsum")
        s_qv = sem("s_qv")
        s_ot = sem("s_ot")
        s_osq = sem("s_osq")
        s_att = sem("s_att")
        s_rms = sem("s_rms")
        s_acc = sem("s_acc")
        s_xs = [sem(f"s_xs{i}") for i in range(2)]
        s_tr = sem("s_tr")
        s_xst = sem("s_xst")
        s_l1 = sem("s_l1")
        s_hb = sem("s_hb")
        s_hg = sem("s_hg")
        s_ht = sem("s_ht")
        s_htc = sem("s_htc")
        s_l2 = sem("s_l2")
        s_yb = sem("s_yb")
        s_ys = [sem(f"s_ys{i}") for i in range(2)]
        s_yg = [sem(f"s_yg{g}") for g in range(G)]
        s_fin = sem("s_fin")
        s_out = sem("s_out")

        x_rows = x_in.rearrange("b t d -> (b t) d").rearrange("(n p) d -> p n d", p=P)
        out_rows = out.rearrange("b t d -> (b t) d").rearrange("(n p) d -> p n d", p=P)

        LAG = 3
        STEPS = TILES + LAG
        LOOPS = (TILES - LAG) // 2

        block = ctx.enter_context(nc.Block())

        @block.sync
        def _(sp):
            for g in range(G):
                sp.dma_start(x_sb[:, g * BPG:(g + 1) * BPG, :], x_rows[:, g * BPG:(g + 1) * BPG, :]).then_inc(s_x[g], 16)
                if g == 0:
                    sp.dma_start(wp[:], wp_in).then_inc(s_wproj, 16)
                    sp.dma_start(wf[:], wf_in).then_inc(s_wproj, 16)
                    sp.dma_start(wi[:], wi_in).then_inc(s_wproj, 16)
                    sp.dma_start(wq[:], wq_in).then_inc(s_wproj, 16)
                    sp.dma_start(bp[:], bp_in.rearrange("(p o) -> p o", o=1)).then_inc(s_wproj, 16)
                    sp.dma_start(cent[:], cent_in).then_inc(s_cent, 16)
            sp.wait_ge(s_zero, 1)
            sp.dma_start(xs_dram.rearrange("(n p) d -> p n d", p=P),
                         zeros[:].unsqueeze(1).to_broadcast([P, TILES, D])).then_inc(s_zfill, 16)
            sp.dma_start(wo[:], wo_in).then_inc(s_wo, 16)
            sp.dma_start(gw[:], gw_in.rearrange("(p o) -> p o", o=1)).then_inc(s_wo, 16)
            sp.dma_start(w1[:], w1_in.rearrange("e d f -> d e f")).then_inc(s_wexp, 16)
            sp.dma_start(w2[:].rearrange("p e (c d) -> p e c d", c=FC),
                         w2_in.rearrange("e (c p) d -> p e c d", p=P)).then_inc(s_wexp, 16)
            sp.dma_start(b1[:].rearrange("p e f -> p (e f)"),
                         b1_in.rearrange("e f -> (e f)").partition_broadcast(P)).then_inc(s_wexp, 16)
            sp.dma_start(b2[:].rearrange("p e f -> p (e f)"),
                         b2_in.rearrange("e f -> (e f)").partition_broadcast(P)).then_inc(s_wexp, 16)

            def load_rows(t, u):
                sp.dma_start(xs[u][:], xs_dram[bass.ds(t * P, P), :]).then_inc(s_xs[u], 16)

            sp.wait_ge(s_sent, 16 * TOPK * NB)
            load_rows(0, 0)
            load_rows(1, 1)
            sp.wait_ge(s_tr, 1)
            load_rows(2, 0)
            with sp.Fori(0, LOOPS) as i:
                for u in range(2):
                    sp.wait_ge(s_tr, 2 * i + 2 + u)
                    load_rows(2 * i + 3 + u, (1 + u) % 2)
            for g in range(G):
                sp.wait_ge(s_fin, g + 1)
                sp.dma_start(out_rows[:, g * BPG:(g + 1) * BPG, :], acc[:, g * BPG:(g + 1) * BPG, :]).then_inc(s_out, 16)
            sp.wait_ge(s_out, 16 * G)

        @block.gpsimd
        def _(pool):
            step = [0]

            def link(ins):
                step[0] += 1
                ins.then_inc(s_const, 1)
                pool.wait_ge(s_const, step[0])

            nc.gpsimd.memset(ones[:], 1.0).then_inc(s_const, 1)
            step[0] += 1
            link(nc.gpsimd.memset(ident[:], 0.0))
            link(nc.gpsimd.affine_select(out=ident[:], in_=ident[:], compare_op=ALU.not_equal, fill=1.0,
                                         base=0, pattern=[[-1, P]], channel_multiplier=1))
            nc.gpsimd.memset(zeros[:], 0.0).then_inc(s_zero, 1)
            link(nc.gpsimd.affine_select(out=before[:], in_=ones[:], compare_op=ALU.is_gt, fill=0.0,
                                         base=0, pattern=[[1, P]], channel_multiplier=-1))
            link(nc.gpsimd.iota(iota_e[:], [[1, E]], base=0, channel_multiplier=0, allow_small_or_imprecise_dtypes=True))
            link(nc.gpsimd.iota(iota_e8[:], [[1, E]], base=E, channel_multiplier=0, allow_small_or_imprecise_dtypes=True))
            link(nc.gpsimd.iota(tile_row[:], [[P, TILES]], base=0, channel_multiplier=0, allow_small_or_imprecise_dtypes=True))
            link(nc.gpsimd.memset(not_first[:], 1.0))
            link(nc.gpsimd.memset(not_first[:, :, 0], 0.0))
            link(nc.gpsimd.memset(v_t[:, :, 0:1], 0.0))
            link(nc.gpsimd.memset(v_t[:, :, T + 1:TP + 1], 0.0))
            link(nc.gpsimd.memset(gate[:, :, 0:1], 0.0))
            link(nc.gpsimd.memset(gate[:, :, T + 1:TP], 0.0))
            ho = head_ones[:].rearrange("p (h d) -> p h d", h=H)
            link(nc.gpsimd.affine_select(out=ho, in_=ones[:].rearrange("p (h d) -> p h d", h=H), compare_op=ALU.is_ge,
                                         fill=0.0, base=0, pattern=[[-DK, H], [0, DK]], channel_multiplier=1))
            link(nc.gpsimd.affine_select(out=ho, in_=ho, compare_op=ALU.is_ge,
                                         fill=0.0, base=DK - 1, pattern=[[DK, H], [0, DK]], channel_multiplier=-1))
            link(nc.gpsimd.affine_select(out=gather[:].rearrange("p j (h d) -> p j h d", h=H),
                                         in_=ho.unsqueeze(1).to_broadcast([P, DK, H, DK]),
                                         compare_op=ALU.is_equal, fill=0.0, base=0,
                                         pattern=[[1, DK], [0, H], [-1, DK]], channel_multiplier=0))
            link(nc.gpsimd.memset(spread_f, 0.0))
            link(nc.gpsimd.affine_select(out=spread_f.rearrange("p j (h d) -> p j h d", h=H),
                                         in_=spread_f.rearrange("p j (h d) -> p j h d", h=H),
                                         compare_op=ALU.not_equal, fill=1.0, base=0,
                                         pattern=[[-1, DK], [-DK, H], [0, DK]], channel_multiplier=1))
            for g in range(G):
                bs = slice(g * GB, (g + 1) * GB)
                pool.wait_ge(s_v, g + 1)
                nc.gpsimd.tensor_tensor(dv_f[:, g % 2], v_t[:, bs, 0:TP], v_t[:, bs, 1:TP + 1], ALU.subtract).then_inc(s_dvf, 1)
                pool.wait_ge(s_dvf, g + 1)
                pool.wait_ge(s_dvh, g + 1)
                nc.gpsimd.tensor_tensor(dv_lo[:, bs, :], dv_f[:, g % 2], dv_hi[:, bs, :].bitcast(F32), ALU.subtract).then_inc(s_dvl, 1)
            pool.wait_ge(s_pos, 1)
            pool.wait_ge(s_zfill, 16)
            for n in range(NB):
                for k in range(TOPK):
                    nc.gpsimd.indirect_dma_start(
                        out=xs_dram, out_offset=bass.IndirectOffsetOnAxis(ap=pos[:, k, n:n + 1], axis=0),
                        in_=xn[:, n, :], in_offset=None).then_inc(s_sent, 16)
            for u in range(2):
                pool.wait_ge(s_ys[u], 16 * ((TILES + 1 - u) // 2))
            for n in range(NB):
                for k in range(TOPK):
                    nc.gpsimd.indirect_dma_start(
                        out=y_rows[:, k, n, :], out_offset=None, in_=ys_dram,
                        in_offset=bass.IndirectOffsetOnAxis(ap=pos[:, k, n:n + 1], axis=0)).then_inc(s_yg[n // BPG], 16)

        IDENT, CONSTS = 3, 18

        @block.scalar
        def _(act):
            for g in range(G):
                bs = slice(g * GB, (g + 1) * GB)
                act.wait_ge(s_xtp, g + 1)
                nc.scalar.copy(xn_t[:, g, :], bank[g % 2][:]).then_inc(s_xnt, 1)
                act.wait_ge(s_wproj, 16 * 5)
                act.wait_ge(s_pp, g + 1)
                if g >= 2:
                    act.wait_ge(s_rp, g - 1)
                nc.scalar.activation(xp_t[:, g % 2], bank[2][:], ACT.Identity, bias=bp[:, 0:1])
                nc.scalar.activation(xp_sq[:, g % 2], bank[2][:], ACT.Square, bias=bp[:, 0:1]).then_inc(s_xp, 1)
                act.wait_ge(s_fp, g + 1)
                if g == 0:
                    act.wait_ge(s_const, CONSTS)
                nc.scalar.activation(gate[:, bs, 1:T + 1], bank[3][:].rearrange("p (b t) -> p b t", b=GB),
                                     ACT.Sigmoid).then_inc(s_gate, 1)
                act.wait_ge(s_ip, g + 1)
                nc.scalar.copy(v_t[:, bs, 1:T + 1], bank[4][:].rearrange("p (b t) -> p b t", b=GB)).then_inc(s_v, 1)
                act.wait_ge(s_qp, g + 1)
                if g >= 2:
                    act.wait_ge(s_q, g - 1)
                nc.scalar.activation(sig_q[:, g % 2], bank[5][:], ACT.Sigmoid).then_inc(s_sigq, 1)
                act.wait_ge(s_dvf, g + 1)
                nc.scalar.copy(dv_hi[:, bs, :], dv_f[:, g % 2]).then_inc(s_dvh, 1)
            act.wait_ge(s_const, CONSTS)
            nc.scalar.copy(spread[:], spread_f).then_inc(s_spread, 1)
            act.wait_ge(s_wo, 32)
            nc.scalar.activation(gwo[:], wo[:], ACT.Copy, scale=gw[:, 0:1]).then_inc(s_gwo, 1)

            def attention(first, last):
                with act.Fori(first, last) as g:
                    act.wait_ge(s_ot, g + 1)
                    nc.scalar.activation(o_sq[:], o_t[:], ACT.Square).then_inc(s_osq, 1)

            def turn(s, u):
                act.wait_ge(s_tr, s + 1)
                nc.scalar.copy(xs_t[u][:], bank[4 + u][:, 0:P]).then_inc(s_xst, 1)

            def gelu(t, u):
                act.wait_ge(s_hb, t + 1)
                nc.scalar.activation(hg[u], hb[u], ACT.Gelu).then_inc(s_hg, 1)

            def turn_hidden(t, u):
                act.wait_ge(s_ht, t + 1)
                nc.scalar.copy(h_t[u][:], bank[2 + u][:]).then_inc(s_htc, 1)

            attention(0, G // 2)
            turn(0, 0)
            turn(1, 1)
            gelu(0, 0)
            act.wait_ge(s_l1, 1)
            turn(2, 0)
            act.wait_ge(s_ht, 1)
            gelu(1, 1)
            turn_hidden(0, 0)

            def store_rows(t, u):
                act.wait_ge(s_yb, t + 1)
                act.dma_start(ys_dram[bass.ds(t * P, P), :], yb[u][:]).then_inc(s_ys[u], 16)

            def steps(i):
                for u in range(2):
                    s = 2 * i + LAG + u
                    act.wait_ge(s_l1, s - 1)
                    turn(s, (LAG + u) % 2)
                    act.wait_ge(s_ht, s - 2)
                    gelu(s - 1, (LAG + u - 1) % 2)
                    if u > 0 or not isinstance(i, int):
                        act.wait_ge(s_l2, s - 3)
                    turn_hidden(s - 2, (LAG + u - 2) % 2)
                    if u > 0 or not isinstance(i, int):
                        store_rows(s - 4, 1 - u)

            steps(0)
            with act.Fori(1, LOOPS) as i:
                steps(i)
            gelu(TILES - 1, (TILES - 1) % 2)
            act.wait_ge(s_l2, TILES - 3)
            turn_hidden(TILES - 2, (TILES - 2) % 2)
            act.wait_ge(s_l2, TILES - 2)
            turn_hidden(TILES - 1, (TILES - 1) % 2)
            for t in range(TILES - 4, TILES):
                store_rows(t, t % 2)
            attention(G // 2, G)

        @block.tensor
        def _(pe):
            pe.wait_ge(s_const, IDENT)

            def turn_group(g):
                pe.wait_ge(s_xn, g + 1)
                if g >= 2:
                    pe.wait_ge(s_xnt, g - 1)
                for j in range(BPG):
                    last = nc.tensor.transpose(bank[g % 2][:, j * P:(j + 1) * P], xn[:, g * BPG + j, :], ident[:])
                last.then_inc(s_xtp, 1)

            turn_group(0)
            pe.wait_ge(s_wproj, 16 * 5)
            for g in range(G):
                if g + 1 < G:
                    turn_group(g + 1)
                pe.wait_ge(s_xnt, g + 1)
                for w, b, done, used in ((wp, 2, s_pp, s_xp), (wf, 3, s_fp, s_gate), (wi, 4, s_ip, s_v), (wq, 5, s_qp, s_q)):
                    if g >= 1:
                        pe.wait_ge(used, g)
                    nc.tensor.matmul(bank[b][:], w[:], xn_t[:, g, :], start=True, stop=True).then_inc(done, 1)
                if g == 0:
                    pe.wait_ge(s_cp, 1)
                    nc.tensor.transpose(bank[6][:, 0:E], cent_p[:], ident[0:E, 0:E]).then_inc(s_cpe, 1)
                    pe.wait_ge(s_cpt, 1)
                    nc.tensor.matmul(bank[6][:, E:2 * E], ones[:], cp_sq[:], start=True, stop=True).then_inc(s_cpe, 1)
                pe.wait_ge(s_xp, g + 1)
                for j in range(BPG):
                    c = (g * BPG + j) * 2 * E
                    nc.tensor.matmul(bank[7][:, c:c + E], xp_t[:, g % 2, j * P:(j + 1) * P], cp_t[:], start=True, stop=True)
                    last = nc.tensor.matmul(bank[7][:, c + E:c + E + 1], xp_sq[:, g % 2, j * P:(j + 1) * P],
                                            ones[:, 0:1], start=True, stop=True)
                last.then_inc(s_rp, 1)
            pe.wait_ge(s_route, 1)
            chosen = r_big[9][:].rearrange("p n e -> p (n e)")
            nc.tensor.matmul(bank[6][:, 0:NB * E], before[:], chosen, start=True, stop=True)
            nc.tensor.matmul(bank[6][:, NB * E:2 * NB * E], ones[:], chosen, start=True, stop=True).then_inc(s_rank, 1)

            def spread_v(n, g, j):
                for b in range(GB):
                    rows = [d[:, bass.ds(g * GB + b, 1), :].rearrange("p o t -> p (o t)") for d in (dv_hi, dv_lo)]
                    ps = bank[2 * (j % 2) + b][:, 0:TP]
                    nc.tensor.matmul(ps, spread[:, j, :], rows[0], start=True, stop=False)
                    last = nc.tensor.matmul(ps, spread[:, j, :], rows[1], start=False, stop=True)
                last.then_inc(s_vb, 1)

            def attention(first, last_g):
                with pe.Fori(first, last_g) as g:
                    nc.tensor.matmul(bank[5][:], head_ones[:], q_t[:, bass.ds(g, 1), :].rearrange("p o t -> p (o t)"), start=True, stop=True).then_inc(s_qsum, 1)
                    spread_v(g * DK, g, 0)
                    spread_v(g * DK + 1, g, 1)
                    for j in range(DK):
                        if j + 2 < DK:
                            pe.wait_ge(s_scan, GB * (g * DK + j + 1))
                            spread_v(g * DK + j + 2, g, j + 2)
                        pe.wait_ge(s_qs, g * DK + j + 1)
                        nc.tensor.matmul(bank[4][:], gather[:, j, :], qstate[:, j % 2], start=(j == 0),
                                         stop=(j == DK - 1)).then_inc(s_red, 1)
                    pe.wait_ge(s_osq, g + 1)
                    for j in range(BPG):
                        nc.tensor.matmul(bank[6][:, j:j + 1], o_sq[:, j * P:(j + 1) * P], ones[:, 0:1], start=True, stop=True)
                    for j in range(BPG):
                        last = nc.tensor.matmul(bank[7][:, j * D:(j + 1) * D], o_t[:, j * P:(j + 1) * P], gwo[:],
                                                start=True, stop=True)
                    last.then_inc(s_att, 1)

            pe.wait_ge(s_const, CONSTS)
            pe.wait_ge(s_q, G)
            pe.wait_ge(s_dvl, G)
            pe.wait_ge(s_spread, 1)
            pe.wait_ge(s_gwo, 1)
            pe.wait_ge(s_pos, 1)
            attention(0, G // 2)

            def turn(s, u):
                nc.tensor.transpose(bank[4 + u][:, 0:P], xs[u][:], ident[:]).then_inc(s_tr, 1)

            def layer1(t, u, e):
                pe.wait_ge(s_xst, t + 1)
                nc.tensor.matmul(bank[u][:], xs_t[u][:], w1[:, bass.ds(e, 1), :].rearrange("p o f -> p (o f)"), start=True, stop=True).then_inc(s_l1, 1)

            def turn_hidden(t, u):
                pe.wait_ge(s_hg, t + 1)
                for c in range(FC):
                    last = nc.tensor.transpose(bank[2 + u][:, c * P:(c + 1) * P], hg[u][:, c * P:(c + 1) * P], ident[:])
                last.then_inc(s_ht, 1)

            def layer2(t, u, e):
                pe.wait_ge(s_htc, t + 1)
                for c in range(FC):
                    last = nc.tensor.matmul(bank[6 + u][:, 0:D], h_t[u][:, c * P:(c + 1) * P],
                                            w2[:, bass.ds(e, 1), c * D:(c + 1) * D].rearrange("p o f -> p (o f)"), start=(c == 0), stop=(c == FC - 1))
                last.then_inc(s_l2, 1)

            def expert(t):
                return pe.value_load(own[0:1, bass.ds(t, 1)], min_val=0, max_val=E - 1)

            pe.wait_ge(s_wexp, 64)
            pe.wait_ge(s_own, 1)
            pe.wait_ge(s_acc, G // 2)
            pe.wait_ge(s_xs[0], 16)
            turn(0, 0)
            pe.wait_ge(s_xs[1], 16)
            turn(1, 1)
            layer1(0, 0, expert(0))
            pe.wait_ge(s_xst, 1)
            pe.wait_ge(s_xs[0], 32)
            turn(2, 0)
            layer1(1, 1, expert(1))
            turn_hidden(0, 0)

            def steps(i):
                for u in range(2):
                    s = 2 * i + LAG + u
                    a, b = (LAG + u) % 2, (LAG + u - 1) % 2
                    pe.wait_ge(s_xs[a], 16 * (i + 2 + u))
                    pe.wait_ge(s_xst, s - 1)
                    turn(s, a)
                    pe.wait_ge(s_hb, s - 2)
                    layer1(s - 1, b, expert(s - 1))
                    turn_hidden(s - 2, a)
                    if u > 0 or not isinstance(i, int):
                        pe.wait_ge(s_yb, s - 3)
                    layer2(s - 3, b, expert(s - 3))

            steps(0)
            with pe.Fori(1, LOOPS) as i:
                steps(i)
            pe.wait_ge(s_hb, TILES - 2)
            layer1(TILES - 1, (TILES - 1) % 2, expert(TILES - 1))
            pe.wait_ge(s_htc, TILES - 3)
            turn_hidden(TILES - 2, (TILES - 2) % 2)
            pe.wait_ge(s_yb, TILES - 3)
            layer2(TILES - 3, (TILES - 3) % 2, expert(TILES - 3))
            pe.wait_ge(s_htc, TILES - 2)
            turn_hidden(TILES - 1, (TILES - 1) % 2)
            pe.wait_ge(s_yb, TILES - 2)
            layer2(TILES - 2, (TILES - 2) % 2, expert(TILES - 2))
            pe.wait_ge(s_yb, TILES - 1)
            layer2(TILES - 1, (TILES - 1) % 2, expert(TILES - 1))
            pe.wait_ge(s_yb, TILES)
            attention(G // 2, G)

        @block.vector
        def _(dve):
            chain = [0]

            def link(ins):
                chain[0] += 1
                ins.then_inc(s_dve, 1)
                dve.wait_ge(s_dve, chain[0])

            V = nc.vector

            def rsqrt(y, x, t, then=link):
                then(V.tensor_scalar(t.bitcast(I32), x.bitcast(I32), 1, None, ALU.logical_shift_right))
                then(V.tensor_scalar(y.bitcast(I32), t.bitcast(I32), -1.0, RSQRT_GUESS, ALU.mult, ALU.add))
                for _ in range(NEWTON):
                    then(V.tensor_tensor(t, y, y, ALU.mult))
                    then(V.scalar_tensor_tensor(out=t, in0=t, scalar=-0.5, in1=x, op0=ALU.mult, op1=ALU.mult))
                    then(V.scalar_tensor_tensor(out=y, in0=t, scalar=1.5, in1=y, op0=ALU.add, op1=ALU.mult))

            def layernorm(g):
                ns = slice(g * BPG, (g + 1) * BPG)
                dve.wait_ge(s_x[g], 16)
                for n in range(g * BPG, (g + 1) * BPG):
                    ins = V.bn_stats(stats[:, n, :], x_sb[:, n, :])
                link(ins)
                for n in range(g * BPG, (g + 1) * BPG):
                    ins = V.bn_aggr(mean_var[:, n, :], stats[:, n, :])
                link(ins)
                link(V.tensor_scalar(var[:, ns], mean_var[:, ns, 1], LN_EPS, None, ALU.add))
                rsqrt(rstd[:, ns], var[:, ns], halves[:, ns])
                for n in range(g * BPG, (g + 1) * BPG):
                    ins = V.tensor_scalar(xn[:, n, :], x_sb[:, n, :], mean_var[:, n, 0:1], rstd[:, n:n + 1],
                                          ALU.subtract, ALU.mult)
                ins.then_inc(s_xn, 1)

            layernorm(0)
            dve.wait_ge(s_cent, 16)
            link(V.tensor_tensor(cent_sq[:], cent[:], cent[:], ALU.mult))
            link(V.tensor_reduce(cent_s[:, 0:1], cent_sq[:], AX.X, ALU.add))
            rsqrt(cent_s[:, 2:3], cent_s[:, 0:1], cent_s[:, 1:2])
            link(V.tensor_scalar(cent_s[:, 3:4], cent_s[:, 2:3], MAX_NORM, 1.0, ALU.mult, ALU.min))
            V.tensor_scalar(cent_p[:], cent[:], cent_s[:, 3:4], None, ALU.mult).then_inc(s_cp, 1)
            layernorm(1)
            dve.wait_ge(s_cpe, 1)
            link(V.tensor_copy(cp_t[:], bank[6][:, 0:E]))
            V.tensor_tensor(cp_sq[:], cp_t[:], cp_t[:], ALU.mult).then_inc(s_cpt, 1)
            for g in range(G):
                if g + 2 < G:
                    layernorm(g + 2)
                dve.wait_ge(s_sigq, g + 1)
                V.scalar_tensor_tensor(out=q_t[:, g, :], in0=bank[5][:], scalar=QSCALE, in1=sig_q[:, g % 2],
                                       op0=ALU.mult, op1=ALU.mult).then_inc(s_q, 1)
            dve.wait_ge(s_cpe, 2)
            link(V.tensor_scalar(c_n2[:], bank[6][:, E:2 * E], NORM_CAP, None, ALU.min))
            link(V.tensor_scalar(c_om[:], c_n2[:], -1.0, 1.0, ALU.mult, ALU.add))

            dve.wait_ge(s_rp, G)
            prod = bank[7][:, 0:NB * 2 * E].rearrange("p (n c) -> p n c", c=2 * E)
            n2 = prod[:, :, E]

            def tok(i):
                return r_tok[i][:].unsqueeze(2).to_broadcast([P, NB, E])

            def exp(a):
                return a[:].unsqueeze(1).to_broadcast([P, NB, E])

            link(V.tensor_copy(r_tok[0][:], n2))
            rsqrt(r_tok[1][:], r_tok[0][:], r_tok[2][:])
            link(V.tensor_scalar(r_tok[2][:], r_tok[1][:], MAX_NORM, 1.0, ALU.mult, ALU.min))
            V.tensor_tensor(r_big[0][:], prod[:, :, 0:E], tok(2), ALU.mult)
            link(V.tensor_tensor(r_tok[3][:], r_tok[0][:], r_tok[2][:], ALU.mult))
            link(V.tensor_tensor(r_tok[4][:], r_tok[3][:], r_tok[2][:], ALU.mult))
            link(V.tensor_scalar(r_tok[5][:], r_tok[4][:], NORM_CAP, None, ALU.min))
            link(V.scalar_tensor_tensor(out=r_big[1][:], in0=r_big[0][:], scalar=-2.0, in1=tok(5), op0=ALU.mult, op1=ALU.add))
            V.tensor_tensor(r_big[2][:], r_big[1][:], exp(c_n2), ALU.add)
            link(V.tensor_scalar(r_tok[6][:], r_tok[5][:], -1.0, 1.0, ALU.mult, ALU.add))
            link(V.tensor_tensor(r_big[3][:], tok(6), exp(c_om), ALU.mult))
            link(V.tensor_scalar(r_big[4][:], r_big[3][:], BALL_EPS, None, ALU.add))
            V.tensor_scalar(r_big[1][:], r_big[2][:], 0.0, 2.0, ALU.max, ALU.mult)
            link(V.reciprocal(r_big[5][:], r_big[4][:]))
            link(V.tensor_tensor(r_big[6][:], r_big[1][:], r_big[5][:], ALU.mult))
            link(V.tensor_scalar(r_big[0][:], r_big[6][:], 1.0, ARG_MIN, ALU.add, ALU.max))
            hot = (r_big[7], r_big[8])
            arg = r_big[0]
            for k in range(TOPK):
                link(V.tensor_reduce(m12[:, k, :], arg[:], AX.X, ALU.min))
                link(V.tensor_tensor(r_big[2][:], arg[:], m12[:, k, :].unsqueeze(2).to_broadcast([P, NB, E]), ALU.is_equal))
                link(V.scalar_tensor_tensor(out=r_big[3][:], in0=r_big[2][:], scalar=-float(E), in1=exp(iota_e8),
                                            op0=ALU.mult, op1=ALU.add))
                link(V.tensor_reduce(r_tok[7][:], r_big[3][:], AX.X, ALU.min))
                link(V.tensor_tensor(hot[k][:], exp(iota_e), tok(7), ALU.is_equal))
                if k == 0:
                    link(V.scalar_tensor_tensor(out=r_big[1][:], in0=hot[0][:], scalar=FAR, in1=arg[:], op0=ALU.mult, op1=ALU.add))
                    arg = r_big[1]
            V.tensor_tensor(r_big[9][:], hot[0][:], hot[1][:], ALU.add).then_inc(s_route, 1)
            link(V.tensor_scalar(u_a[:], m12[:], 1.0, None, ALU.subtract))
            link(V.scalar_tensor_tensor(out=u_b[:], in0=m12[:], scalar=1.0, in1=u_a[:], op0=ALU.add, op1=ALU.mult))
            rsqrt(u_a[:], u_b[:], u_c[:])
            link(V.tensor_tensor(u_c[:], u_a[:], u_b[:], ALU.mult))
            link(V.tensor_tensor(u_b[:], u_c[:], m12[:], ALU.add))
            link(V.reciprocal(u_a[:, 1, :], u_b[:, 1, :]))
            link(V.tensor_tensor(r_tok[0][:], u_b[:, 0, :], u_a[:, 1, :], ALU.mult))
            link(V.tensor_scalar(r_tok[1][:], r_tok[0][:], 1.0, None, ALU.add))
            link(V.reciprocal(weight[:, 0, :], r_tok[1][:]))
            link(V.tensor_tensor(weight[:, 1, :], r_tok[0][:], weight[:, 0, :], ALU.mult))
            dve.wait_ge(s_rank, 1)
            rank = bank[6][:, 0:NB * E].rearrange("p (n e) -> p e n", e=E)
            total = bank[6][:, NB * E:2 * NB * E].rearrange("p (n e) -> p e n", e=E)
            link(V.tensor_copy(tot[:], total))
            link(V.tensor_tensor_scan(inc[:].rearrange("p e n -> p (e n)"), not_first[:].rearrange("p e n -> p (e n)"),
                                      tot[:].rearrange("p e n -> p (e n)"), 0.0, ALU.mult, ALU.add))
            V.tensor_tensor(exc[:], inc[:], tot[:], ALU.subtract)
            link(V.tensor_scalar(cnt_i[:, 0, :], inc[:, :, NB - 1], float(P - 1), None, ALU.add))
            SH = P.bit_length() - 1
            link(V.tensor_scalar(cnt_i[:, 1, :], cnt_i[:, 0, :], SH, SH, ALU.logical_shift_right, ALU.logical_shift_left))
            link(V.tensor_copy(pad_f[:, 0, :], cnt_i[:, 1, :]))
            link(V.tensor_tensor_scan(pad_f[:, 1, :], ones[:, 0:E], pad_f[:, 0, :], 0.0, ALU.mult, ALU.add))
            link(V.tensor_tensor(pad_f[:, 2, :], pad_f[:, 1, :], pad_f[:, 0, :], ALU.subtract))
            link(V.tensor_tensor(tot[:], exc[:], pad_f[:, 2, :].unsqueeze(2).to_broadcast([P, E, NB]), ALU.add))
            link(V.tensor_tensor(inc[:], rank, tot[:], ALU.add))
            for k in range(TOPK):
                link(V.tensor_tensor(r_big[2][:], hot[k][:], inc[:].rearrange("p e n -> p n e"), ALU.mult))
                link(V.tensor_reduce(pos_f[:, k, :], r_big[2][:], AX.X, ALU.add))
            V.tensor_copy(pos[:], pos_f[:]).then_inc(s_pos, 1)
            link(V.tensor_tensor(own_f[:], pad_f[0:1, 1, :].unsqueeze(1).to_broadcast([1, TILES, E]),
                                 tile_row[:].unsqueeze(2).to_broadcast([1, TILES, E]), ALU.is_le))
            link(V.tensor_reduce(own_s[:, 0, :], own_f[:], AX.X, ALU.add))
            link(V.tensor_scalar(own_s[:, 1, :], own_s[:, 0, :], float(E - 1), None, ALU.min))
            V.tensor_copy(own[:, 0:TILES], own_s[:, 1, :]).then_inc(s_own, 1)

            def scans(n, g, j):
                dve.wait_ge(s_vb, n + 1)
                if j >= 3:
                    dve.wait_ge(s_qs, n - 2)
                for b in range(GB):
                    V.tensor_tensor_scan(state[:, j % 3, b, :], gate[:, bass.ds(g * GB + b, 1), :].rearrange("p o t -> p (o t)"), bank[2 * (j % 2) + b][:, 0:TP],
                                         0.0, ALU.mult, ALU.add).then_inc(s_scan, 1)

            def times_q(n, g, j):
                dve.wait_ge(s_scan, GB * (n + 1))
                if j >= 2:
                    dve.wait_ge(s_red, n - 1)
                V.tensor_tensor(qstate[:, j % 2].rearrange("p (b t) -> p b t", b=GB), state[:, j % 3, :, 1:T + 1],
                                q_t[:, bass.ds(g, 1), :].rearrange("p o (b t) -> p (o b) t", b=GB),
                                ALU.mult).then_inc(s_qs, 1)

            def attention(first, last):
                with dve.Fori(first, last) as g:
                    scans(g * DK, g, 0)
                    dve.wait_ge(s_qsum, g + 1)
                    V.tensor_tensor(q_v[:].rearrange("p (b t) -> p b t", b=GB), bank[5][:].rearrange("p (b t) -> p b t", b=GB),
                                    v_t[:, bass.ds(g * GB, GB), 2:T + 2], ALU.mult).then_inc(s_qv, 1)
                    for j in range(DK):
                        if j + 1 < DK:
                            scans(g * DK + j + 1, g, j + 1)
                        times_q(g * DK + j, g, j)
                    dve.wait_ge(s_red, (g + 1) * DK)
                    dve.wait_ge(s_qv, g + 1)
                    V.tensor_tensor(o_t[:], bank[4][:], q_v[:], ALU.add).then_inc(s_ot, 1)
                    dve.wait_ge(s_att, g + 1)
                    done = [0]

                    def link_rms(ins):
                        done[0] += 1
                        ins.then_inc(s_rms, 1)
                        dve.wait_ge(s_rms, RMS_STEPS * g + done[0])

                    link_rms(V.tensor_scalar(rms[:, 0, :], bank[6][:, 0:BPG], 1.0 / D, RMS_EPS, ALU.mult, ALU.add))
                    rsqrt(rms[:, 1, :], rms[:, 0, :], rms[:, 2, :], link_rms)
                    assert done[0] == RMS_STEPS
                    for j in range(BPG):
                        n = bass.ds(g * BPG + j, 1)
                        ins = V.scalar_tensor_tensor(out=acc[:, n, :].rearrange("p o d -> p (o d)"), in0=bank[7][:, j * D:(j + 1) * D], scalar=rms[:, 1, j:j + 1],
                                                     in1=x_sb[:, n, :].rearrange("p o d -> p (o d)"), op0=ALU.mult, op1=ALU.add)
                    ins.then_inc(s_acc, 1)

            dve.wait_ge(s_gate, G)
            attention(0, G // 2)

            def bias1(t, u, e):
                dve.wait_ge(s_l1, t + 1)
                V.tensor_tensor(hb[u], bank[u][:], b1[:, bass.ds(e, 1), :].rearrange("p o f -> p (o f)"), ALU.add).then_inc(s_hb, 1)

            def bias2(t, u, e):
                dve.wait_ge(s_l2, t + 1)
                V.tensor_tensor(yb[u][:], bank[6 + u][:, 0:D], b2[:, bass.ds(e, 1), :].rearrange("p o f -> p (o f)"), ALU.add).then_inc(s_yb, 1)

            def expert(t):
                return dve.value_load(own[0:1, bass.ds(t, 1)], min_val=0, max_val=E - 1)

            dve.wait_ge(s_wexp, 64)
            dve.wait_ge(s_own, 1)
            bias1(0, 0, expert(0))
            bias1(1, 1, expert(1))

            def steps(i):
                for u in range(2):
                    s = 2 * i + LAG + u
                    b = (LAG + u - 1) % 2
                    dve.wait_ge(s_hg, s - 2)
                    bias1(s - 1, b, expert(s - 1))
                    if not isinstance(i, int):
                        dve.wait_ge(s_ys[b], 16 * i)
                    bias2(s - 3, b, expert(s - 3))

            steps(0)
            with dve.Fori(1, LOOPS) as i:
                steps(i)
            dve.wait_ge(s_hg, TILES - 2)
            bias1(TILES - 1, (TILES - 1) % 2, expert(TILES - 1))
            for t in range(TILES - 3, TILES):
                dve.wait_ge(s_ys[t % 2], 16 * (t // 2))
                bias2(t, t % 2, expert(t))
            attention(G // 2, G)
            dve.wait_ge(s_acc, G)
            for g in range(G):
                dve.wait_ge(s_yg[g], 16 * TOPK * BPG)
                for k in range(TOPK):
                    for n in range(g * BPG, (g + 1) * BPG):
                        ins = V.scalar_tensor_tensor(out=acc[:, n, :], in0=y_rows[:, k, n, :], scalar=weight[:, k, n:n + 1],
                                                     in1=acc[:, n, :], op0=ALU.mult, op1=ALU.add)
                    if k + 1 < TOPK:
                        link(ins)
                ins.then_inc(s_fin, 1)


_INS = ["L0_attn_hidden_states", "L0_attn_Wq", "L0_attn_Wf", "L0_attn_Wi", "L0_attn_g_weight", "L0_attn_Wo",
        "L0_ffn_centroids", "L0_ffn_Wp", "L0_ffn_bp", "L0_ffn_W1", "L0_ffn_b1", "L0_ffn_W2", "L0_ffn_b2"]


def kernel(**inputs):
    import numpy as _np
    import concourse.bacc as _bacc
    from concourse import mybir as _mybir
    from concourse.bass_utils import run_bass_kernel_spmd as _run

    nc = _bacc.Bacc("TRN2", target_bir_lowering=False, num_devices=1)
    arrays, args = {}, []
    for name in _INS:
        a = _np.ascontiguousarray(inputs[name])
        arrays[f"in_{name}_dram"] = a
        args.append(nc.dram_tensor(f"in_{name}_dram", a.shape, _mybir.dt.from_np(a.dtype), kind="ExternalInput").ap())
    shape = inputs["L0_attn_hidden_states"].shape
    args.append(nc.dram_tensor("out_0_dram", shape, _mybir.dt.float32, kind="ExternalOutput").ap())
    gla_and_routed_experts(nc, *args)
    r = _run(nc, [arrays], core_ids=[0])
    return r.results[0]["out_0_dram"]
```

```python
from contextlib import ExitStack

import numpy as np
import concourse.bass as bass
from concourse import mybir

F32 = mybir.dt.float32
F32R = mybir.dt.float32r
I32 = mybir.dt.int32
U32 = mybir.dt.uint32
ALU = mybir.AluOpType
ACT = mybir.ActivationFunctionType
AX = mybir.AxisListType

P = 128


def gla_and_routed_experts(
    nc: bass.Bass,
    x_in: bass.AP,
    wq_in: bass.AP,
    wf_in: bass.AP,
    wi_in: bass.AP,
    gw_in: bass.AP,
    wo_in: bass.AP,
    cent_in: bass.AP,
    wp_in: bass.AP,
    bp_in: bass.AP,
    w1_in: bass.AP,
    b1_in: bass.AP,
    w2_in: bass.AP,
    b2_in: bass.AP,
    out: bass.AP,
):
    BATCH, T, D = x_in.shape
    H = 8
    DK = D // H
    E, _, F = w1_in.shape
    N = BATCH * T
    NB = N // P
    GB = 2
    G = BATCH // GB
    GT = GB * T
    BPG = GT // P
    TOPK = 2
    TILES = (N * TOPK + E * (P - 1)) // P
    FC = F // P
    RING = 4
    TP = T + 2
    LN_EPS = RMS_EPS = 1e-5
    MAX_NORM, BALL_EPS, NORM_CAP = 0.95, 1e-7, 0.99
    ARG_MIN = float(np.float32(1.0) + np.float32(BALL_EPS))
    FAR = 1e30
    RSQRT_GUESS = float(0x5F3759DF)
    NEWTON = 3
    RMS_STEPS = 3 + 3 * NEWTON
    RANK_AT = 6
    QSCALE = float(DK) ** -0.5
    assert D == P and GT == 512 and F == 512 and TILES == 39 and DK * H == D

    ROWS_OUT = TOPK * N
    xs_dram = nc.dram_tensor("rows_by_expert", (TILES * P, D + 1), F32).ap()
    ys_dram = nc.dram_tensor("expert_rows_out", (ROWS_OUT, D), F32).ap()

    with ExitStack() as ctx:
        def sb(name, shape, dt=F32):
            return ctx.enter_context(nc.sbuf_tensor(name, shape, dt))

        def sem(name):
            return ctx.enter_context(nc.semaphore(name))

        bank = [ctx.enter_context(nc.psum_tensor(f"bank{i}", [P, 512], F32)) for i in range(8)]

        x_sb = sb("x_sb", [P, NB, D])
        xn = sb("xn", [P, NB, D + 1])
        xn_t = sb("xn_t", [P, G, GT])
        acc = x_sb
        stats = sb("stats", [P, NB, 6])
        mean_var = sb("mean_var", [P, NB, 2])
        var = sb("var", [P, NB])
        rstd = sb("rstd", [P, NB])
        halves = sb("halves", [P, NB])

        wq = sb("wq", [P, D])
        wf = sb("wf", [P, D])
        wi = sb("wi", [P, D])
        wp = sb("wp", [P, D])
        wo = sb("wo", [P, D])
        gwo = sb("gwo", [P, D])
        gw = sb("gw", [P, 1])
        bp = sb("bp", [P, 1])
        w1 = sb("w1", [P, E, F])
        w2 = sb("w2", [P, E, FC * D])
        b1_rows = sb("b1_rows", [E * FC, P])
        b1 = sb("b1", [P, E, FC])
        b2 = sb("b2", [P, E, D])

        ident = sb("ident", [P, P])
        ones = sb("ones", [P, P])
        before = sb("before", [P, P])
        head_ones = sb("head_ones", [P, D])
        spread = sb("spread", [P, DK, D], F32R)
        gather = sb("gather", [P, DK, D])
        no_rows = sb("no_rows", [P, D + 1])
        iota_e = sb("iota_e", [P, E])
        iota_e8 = sb("iota_e8", [P, E])
        tile_row = sb("tile_row", [1, TILES])
        not_first = sb("not_first", [P, E, NB])

        q_t = sb("q_t", [P, G, GT])
        gate = sb("gate", [P, BATCH, TP])
        v_t = sb("v_t", [P, BATCH, TP + 1])
        dv_f = sb("dv_f", [P, 2, GB, TP])
        dv_hi = sb("dv_hi", [P, BATCH, TP], F32R)
        dv_lo = sb("dv_lo", [P, BATCH, TP], F32R)
        sig_q = sb("sig_q", [P, 2, GT])
        state = sb("state", [P, 4, GB, TP])
        qstate = sb("qstate", [P, 2, GT])
        q_v = sb("q_v", [P, GT])
        o_t = sb("o_t", [P, GT])
        o_sq = sb("o_sq", [P, GT])
        rms = sb("rms", [P, 3, BPG])

        xp_t = sb("xp_t", [P, 2, GT])
        xp_sq = sb("xp_sq", [P, 2, GT])
        cent = sb("cent", [E, D])
        cent_sq = sb("cent_sq", [E, D])
        cent_p = sb("cent_p", [E, D])
        cent_s = sb("cent_s", [E, 4])
        cp_t = sb("cp_t", [P, E])
        cp_sq = sb("cp_sq", [P, E])
        c_n2 = sb("c_n2", [P, E])
        c_om = sb("c_om", [P, E])
        prod = sb("prod", [P, NB, E + 1])
        r_tok = [sb(f"r_tok{i}", [P, NB]) for i in range(8)]
        r_big = [sb(f"r_big{i}", [P, NB, E]) for i in range(10)]
        m12 = sb("m12", [P, TOPK, NB])
        u_a = sb("u_a", [P, TOPK, NB])
        u_b = sb("u_b", [P, TOPK, NB])
        u_c = sb("u_c", [P, TOPK, NB])
        weight = sb("weight", [P, TOPK, NB])
        tot = sb("tot", [P, E, NB])
        inc = sb("inc", [P, E, NB])
        exc = sb("exc", [P, E, NB])
        cnt_i = sb("cnt_i", [P, 2, E], I32)
        pad_f = sb("pad_f", [P, 3, E])
        pos_f = sb("pos_f", [P, TOPK, NB])
        pos = sb("pos", [P, TOPK, NB], U32)
        own_f = sb("own_f", [1, TILES, E])
        own_s = sb("own_s", [1, 2, TILES])
        own = sb("own", [1, TILES + 1], I32)

        xs = [sb(f"xs{i}", [P, D + 1]) for i in range(RING)]
        place = [sb(f"place{i}", [P, 1], U32) for i in range(RING)]
        place_y = [sb(f"place_y{i}", [P, 1], U32) for i in range(RING)]
        w1_now = [sb(f"w1_now{i}", [P, F]) for i in range(2)]
        xs_t = [sb(f"xs_t{i}", [P, P]) for i in range(2)]
        hg = [xn_t[:, i, :] for i in range(RING)]
        hb = [sb(f"hb{i}", [P, F]) for i in range(2)]
        yb = [sb(f"yb{i}", [P, D]) for i in range(RING)]
        y_rows = sb("y_rows", [P, TOPK, NB, D])
        spread_f = y_rows[:, 0, :, :]

        s_x = [sem(f"s_x{g}") for g in range(G)]
        s_wproj = sem("s_wproj")
        s_wexp = sem("s_wexp")
        s_wo = sem("s_wo")
        s_cent = sem("s_cent")
        s_const = sem("s_const")
        s_zero = sem("s_zero")
        s_zfill = sem("s_zfill")
        s_dve = sem("s_dve")
        s_xn = sem("s_xn")
        s_xtp = sem("s_xtp")
        s_xnt = sem("s_xnt")
        s_pp = sem("s_pp")
        s_fp = sem("s_fp")
        s_ip = sem("s_ip")
        s_qp = sem("s_qp")
        s_xp = sem("s_xp")
        s_rp = sem("s_rp")
        s_gate = sem("s_gate")
        s_v = sem("s_v")
        s_sigq = sem("s_sigq")
        s_q = sem("s_q")
        s_dvf = sem("s_dvf")
        s_dvh = sem("s_dvh")
        s_dvl = sem("s_dvl")
        s_spread = sem("s_spread")
        s_gwo = sem("s_gwo")
        s_cp = sem("s_cp")
        s_cpt = sem("s_cpt")
        s_cpe = sem("s_cpe")
        s_route = sem("s_route")
        s_rank = sem("s_rank")
        s_pos = sem("s_pos")
        s_own = sem("s_own")
        s_sent = sem("s_sent")
        s_vb = sem("s_vb")
        s_scan = sem("s_scan")
        s_qs = sem("s_qs")
        s_red = sem("s_red")
        s_qsum = sem("s_qsum")
        s_qv = sem("s_qv")
        s_ot = sem("s_ot")
        s_osq = sem("s_osq")
        s_att = sem("s_att")
        s_rms = sem("s_rms")
        s_acc = sem("s_acc")
        s_xs = [sem(f"s_xs{i}") for i in range(RING)]
        s_place = sem("s_place")
        s_w1 = sem("s_w1")
        s_b1t = sem("s_b1t")
        s_b1 = sem("s_b1")
        s_b1in = sem("s_b1in")
        s_ids = sem("s_ids")
        s_tr = sem("s_tr")
        s_xst = sem("s_xst")
        s_l1 = sem("s_l1")
        s_hb = sem("s_hb")
        s_hg = sem("s_hg")
        s_l2 = sem("s_l2")
        s_yb = sem("s_yb")
        s_ys = [sem(f"s_ys{i}") for i in range(RING)]
        s_yg = [sem(f"s_yg{g}") for g in range(G)]
        s_fin = sem("s_fin")
        s_out = sem("s_out")

        x_rows = x_in.rearrange("b t d -> (b t) d").rearrange("(n p) d -> p n d", p=P)
        out_rows = out.rearrange("b t d -> (b t) d").rearrange("(n p) d -> p n d", p=P)

        LAG = 3
        ROUNDS = (TILES - LAG) // RING
        assert ROUNDS * RING + LAG == TILES

        serial = iter(range(1 << 20))
        block = ctx.enter_context(nc.Block())

        @block.sync
        def _(sp):
            sp.dma_start(cent[:], cent_in).then_inc(s_cent, 16)
            for g in range(G):
                sp.dma_start(x_sb[:, g * BPG:(g + 1) * BPG, :], x_rows[:, g * BPG:(g + 1) * BPG, :]).then_inc(s_x[g], 16)
                if g == 0:
                    sp.dma_start(b1_rows[:], b1_in.rearrange("e (c p) -> (e c) p", p=P)).then_inc(s_b1in, 16)
                    sp.dma_start(wp[:], wp_in).then_inc(s_wproj, 16)
                    sp.dma_start(wf[:], wf_in).then_inc(s_wproj, 16)
                    sp.dma_start(wi[:], wi_in).then_inc(s_wproj, 16)
                    sp.dma_start(wq[:], wq_in).then_inc(s_wproj, 16)
                    sp.dma_start(bp[:], bp_in.rearrange("(p o) -> p o", o=1)).then_inc(s_wproj, 16)
            sp.wait_ge(s_zero, 1)
            sp.dma_start(xs_dram.rearrange("(n p) d -> p n d", p=P),
                         no_rows[:].unsqueeze(1).to_broadcast([P, TILES, D + 1])).then_inc(s_zfill, 16)
            sp.dma_start(wo[:], wo_in).then_inc(s_wo, 16)
            sp.dma_start(gw[:], gw_in.rearrange("(p o) -> p o", o=1)).then_inc(s_wo, 16)
            sp.dma_start(w1[:], w1_in.rearrange("e d f -> d e f")).then_inc(s_wexp, 16)
            sp.dma_start(w2[:].rearrange("p e (c d) -> p e c d", c=FC),
                         w2_in.rearrange("e (c p) d -> p e c d", p=P)).then_inc(s_wexp, 16)
            sp.dma_start(b2[:].rearrange("p e f -> p (e f)"),
                         b2_in.rearrange("e f -> (e f)").partition_broadcast(P)).then_inc(s_wexp, 16)

            def load_rows(t, u):
                sp.dma_start(xs[u][:], xs_dram[bass.ds(t * P, P), :]).then_inc(s_xs[u], 16)

            sp.wait_ge(s_sent, 16 * TOPK * NB)
            for t in range(RING):
                load_rows(t, t)
            with sp.Fori(1, ROUNDS) as i:
                for u in range(RING):
                    t = RING * i + u
                    sp.wait_ge(s_tr, t - RING + 1)
                    sp.wait_ge(s_place, t - RING + 1)
                    load_rows(t, u)
            for t in range(RING * ROUNDS, TILES):
                sp.wait_ge(s_tr, t - RING + 1)
                sp.wait_ge(s_place, t - RING + 1)
                load_rows(t, t % RING)
            for u in range(RING):
                sp.wait_ge(s_ys[u], 16 * len(range(u, TILES, RING)))
            ys_rows = ys_dram.rearrange("(k n p) d -> p k n d", k=TOPK, p=P)
            for g in range(G):
                for k in range(TOPK):
                    sp.dma_start(y_rows[:, k, g * BPG:(g + 1) * BPG, :], ys_rows[:, k, g * BPG:(g + 1) * BPG, :]).then_inc(s_yg[g], 16)
            for g in range(G):
                sp.wait_ge(s_fin, g + 1)
                sp.dma_start(out_rows[:, g * BPG:(g + 1) * BPG, :], acc[:, g * BPG:(g + 1) * BPG, :]).then_inc(s_out, 16)
            sp.wait_ge(s_out, 16 * G)

        @block.gpsimd
        def _(pool):
            step = [0]

            def link(ins):
                step[0] += 1
                ins.then_inc(s_const, 1)
                pool.wait_ge(s_const, step[0])

            nc.gpsimd.memset(ones[:], 1.0).then_inc(s_const, 1)
            step[0] += 1
            link(nc.gpsimd.memset(ident[:], 0.0))
            link(nc.gpsimd.affine_select(out=ident[:], in_=ident[:], compare_op=ALU.not_equal, fill=1.0,
                                         base=0, pattern=[[-1, P]], channel_multiplier=1))
            link(nc.gpsimd.memset(no_rows[:, 0:D], 0.0))
            nc.gpsimd.memset(no_rows[:, D:D + 1].bitcast(I32), ROWS_OUT).then_inc(s_zero, 1)
            link(nc.gpsimd.affine_select(out=before[:], in_=ones[:], compare_op=ALU.is_gt, fill=0.0,
                                         base=0, pattern=[[1, P]], channel_multiplier=-1))
            link(nc.gpsimd.iota(iota_e[:], [[1, E]], base=0, channel_multiplier=0, allow_small_or_imprecise_dtypes=True))
            link(nc.gpsimd.iota(iota_e8[:], [[1, E]], base=E, channel_multiplier=0, allow_small_or_imprecise_dtypes=True))
            link(nc.gpsimd.iota(tile_row[:], [[P, TILES]], base=0, channel_multiplier=0, allow_small_or_imprecise_dtypes=True))
            link(nc.gpsimd.memset(not_first[:], 1.0))
            link(nc.gpsimd.memset(not_first[:, :, 0], 0.0))
            link(nc.gpsimd.memset(v_t[:, :, 0:1], 0.0))
            link(nc.gpsimd.memset(v_t[:, :, T + 1:TP + 1], 0.0))
            link(nc.gpsimd.memset(gate[:, :, 0:1], 0.0))
            link(nc.gpsimd.memset(gate[:, :, T + 1:TP], 0.0))
            ho = head_ones[:].rearrange("p (h d) -> p h d", h=H)
            link(nc.gpsimd.affine_select(out=ho, in_=ones[:].rearrange("p (h d) -> p h d", h=H), compare_op=ALU.is_ge,
                                         fill=0.0, base=0, pattern=[[-DK, H], [0, DK]], channel_multiplier=1))
            link(nc.gpsimd.affine_select(out=ho, in_=ho, compare_op=ALU.is_ge,
                                         fill=0.0, base=DK - 1, pattern=[[DK, H], [0, DK]], channel_multiplier=-1))
            link(nc.gpsimd.affine_select(out=gather[:].rearrange("p j (h d) -> p j h d", h=H),
                                         in_=ho.unsqueeze(1).to_broadcast([P, DK, H, DK]),
                                         compare_op=ALU.is_equal, fill=0.0, base=0,
                                         pattern=[[1, DK], [0, H], [-1, DK]], channel_multiplier=0))
            link(nc.gpsimd.memset(spread_f, 0.0))
            link(nc.gpsimd.affine_select(out=spread_f.rearrange("p j (h d) -> p j h d", h=H),
                                         in_=spread_f.rearrange("p j (h d) -> p j h d", h=H),
                                         compare_op=ALU.not_equal, fill=1.0, base=0,
                                         pattern=[[-1, DK], [-DK, H], [0, DK]], channel_multiplier=1))
            for g in range(G):
                bs = slice(g * GB, (g + 1) * GB)
                pool.wait_ge(s_v, g + 1)
                nc.gpsimd.tensor_tensor(dv_f[:, g % 2], v_t[:, bs, 0:TP], v_t[:, bs, 1:TP + 1], ALU.subtract).then_inc(s_dvf, 1)
                pool.wait_ge(s_dvf, g + 1)
                pool.wait_ge(s_dvh, g + 1)
                nc.gpsimd.tensor_tensor(dv_lo[:, bs, :], dv_f[:, g % 2], dv_hi[:, bs, :].bitcast(F32), ALU.subtract).then_inc(s_dvl, 1)
            pool.wait_ge(s_xn, G)
            for k in range(TOPK):
                if k > 0:
                    pool.wait_ge(s_sent, 16 * k * NB)
                nc.gpsimd.iota(xn[:, :, D].bitcast(I32), [[P, NB]], base=k * N, channel_multiplier=1).then_inc(s_ids, 1)
                pool.wait_ge(s_ids, k + 1)
                if k == 0:
                    pool.wait_ge(s_pos, 1)
                    pool.wait_ge(s_zfill, 16)
                for n in range(NB):
                    nc.gpsimd.indirect_dma_start(
                        out=xs_dram, out_offset=bass.IndirectOffsetOnAxis(ap=pos[:, k, n:n + 1], axis=0),
                        in_=xn[:, n, :], in_offset=None).then_inc(s_sent, 16)

            last_row = pool.alloc_register("last_row")
            limit = pool.alloc_register("limit")
            pool.reg_mov(last_row, ROWS_OUT - 1)

            def return_rows(t, u):
                pool.wait_ge(s_yb, t + 1)
                pool.reg_add(limit, last_row, 0)
                nc.gpsimd.indirect_dma_start(
                    out=ys_dram, out_offset=bass.IndirectOffsetOnAxis(ap=place_y[u][:, 0:1], axis=0),
                    in_=yb[u][:], in_offset=None, bounds_check=pool.snap(limit, min_val=0, max_val=ROWS_OUT - 1), oob_is_err=False).then_inc(s_ys[u], 16)

            with pool.Fori(0, ROUNDS) as i:
                for u in range(RING):
                    return_rows(RING * i + u, u)
            for t in range(RING * ROUNDS, TILES):
                return_rows(t, t % RING)

        IDENT, CONSTS = 3, 19

        @block.scalar
        def _(act):
            for g in range(G):
                bs = slice(g * GB, (g + 1) * GB)
                act.wait_ge(s_xtp, g + 1)
                nc.scalar.copy(xn_t[:, g, :], bank[g % 2][:]).then_inc(s_xnt, 1)
                act.wait_ge(s_wproj, 16 * 5)
                act.wait_ge(s_pp, g + 1)
                if g >= 2:
                    act.wait_ge(s_rp, g - 1)
                nc.scalar.activation(xp_t[:, g % 2], bank[2][:], ACT.Identity, bias=bp[:, 0:1])
                nc.scalar.activation(xp_sq[:, g % 2], bank[2][:], ACT.Square, bias=bp[:, 0:1]).then_inc(s_xp, 1)
                act.wait_ge(s_fp, g + 1)
                if g == 0:
                    act.wait_ge(s_const, CONSTS)
                nc.scalar.activation(gate[:, bs, 1:T + 1], bank[3][:].rearrange("p (b t) -> p b t", b=GB),
                                     ACT.Sigmoid).then_inc(s_gate, 1)
                act.wait_ge(s_ip, g + 1)
                nc.scalar.copy(v_t[:, bs, 1:T + 1], bank[4][:].rearrange("p (b t) -> p b t", b=GB)).then_inc(s_v, 1)
                act.wait_ge(s_qp, g + 1)
                if g >= 2:
                    act.wait_ge(s_q, g - 1)
                nc.scalar.activation(sig_q[:, g % 2], bank[5][:], ACT.Sigmoid).then_inc(s_sigq, 1)
                act.wait_ge(s_dvf, g + 1)
                nc.scalar.copy(dv_hi[:, bs, :], dv_f[:, g % 2]).then_inc(s_dvh, 1)
            act.wait_ge(s_const, CONSTS)
            nc.scalar.copy(spread[:], spread_f).then_inc(s_spread, 1)
            act.wait_ge(s_wo, 32)
            nc.scalar.activation(gwo[:], wo[:], ACT.Copy, scale=gw[:, 0:1]).then_inc(s_gwo, 1)

            def attention(g):
                act.wait_ge(s_ot, g + 1)
                nc.scalar.activation(o_sq[:], o_t[:], ACT.Square).then_inc(s_osq, 1)

            def turn(s, u):
                act.wait_ge(s_tr, s + 1)
                nc.scalar.copy(xs_t[u % 2][:], bank[4 + u % 2][:, 0:P]).then_inc(s_xst, 1)

            def gelu(t, u):
                act.wait_ge(s_hb, t + 1)
                nc.scalar.activation(hg[u], hb[u % 2][:], ACT.Gelu).then_inc(s_hg, 1)

            attention(0)
            with act.Fori(1, G - 1) as g:
                attention(g)
            turn(0, 0)
            turn(1, 1)
            gelu(0, 0)
            act.wait_ge(s_l1, 1)
            turn(2, 2)
            gelu(1, 1)

            def steps(i):
                for u in range(RING):
                    s = RING * i + LAG + u
                    act.wait_ge(s_l1, s - 1)
                    turn(s, (LAG + u) % RING)
                    if not isinstance(s, int) or s > 4:
                        act.wait_ge(s_l2, s - 4)
                    gelu(s - 1, (LAG + u - 1) % RING)

            steps(0)
            with act.Fori(1, ROUNDS) as i:
                steps(i)
            act.wait_ge(s_l2, TILES - 4)
            gelu(TILES - 1, (TILES - 1) % RING)
            attention(G - 1)

        @block.tensor
        def _(pe):
            pe.wait_ge(s_const, IDENT)

            def turn_group(g):
                pe.wait_ge(s_xn, g + 1)
                if g >= 2:
                    pe.wait_ge(s_xnt, g - 1)
                for j in range(BPG):
                    last = nc.tensor.transpose(bank[g % 2][:, j * P:(j + 1) * P], xn[:, g * BPG + j, 0:D], ident[:])
                last.then_inc(s_xtp, 1)

            pe.wait_ge(s_cp, 1)
            nc.tensor.transpose(bank[6][:, 0:E], cent_p[:], ident[0:E, 0:E]).then_inc(s_cpe, 1)
            turn_group(0)
            pe.wait_ge(s_cpt, 1)
            nc.tensor.matmul(bank[6][:, E:2 * E], ones[:], cp_sq[:], start=True, stop=True).then_inc(s_cpe, 1)
            pe.wait_ge(s_b1in, 16)
            nc.tensor.transpose(bank[6][:, 2 * E:2 * E + E * FC], b1_rows[:], ident[0:E * FC, 0:E * FC]).then_inc(s_b1t, 1)
            pe.wait_ge(s_wproj, 16 * 5)
            for g in range(G):
                pe.wait_ge(s_xnt, g + 1)
                for w, b, done, used in ((wp, 2, s_pp, s_xp), (wf, 3, s_fp, s_gate), (wi, 4, s_ip, s_v), (wq, 5, s_qp, s_q)):
                    if g >= 1:
                        pe.wait_ge(used, g)
                    nc.tensor.matmul(bank[b][:], w[:], xn_t[:, g, :], start=True, stop=True).then_inc(done, 1)
                if g + 1 < G:
                    turn_group(g + 1)
                pe.wait_ge(s_xp, g + 1)
                for j in range(BPG):
                    c = (g * BPG + j) * 2 * E
                    nc.tensor.matmul(bank[7][:, c:c + E], xp_t[:, g % 2, j * P:(j + 1) * P], cp_t[:], start=True, stop=True)
                    last = nc.tensor.matmul(bank[7][:, c + E:c + E + 1], xp_sq[:, g % 2, j * P:(j + 1) * P],
                                            ones[:, 0:1], start=True, stop=True)
                last.then_inc(s_rp, 1)

            def ranks():
                pe.wait_ge(s_route, 1)
                chosen = r_big[9][:].rearrange("p n e -> p (n e)")
                nc.tensor.matmul(bank[6][:, 0:NB * E], before[:], chosen, start=True, stop=True)
                nc.tensor.matmul(bank[6][:, NB * E:2 * NB * E], ones[:], chosen, start=True, stop=True).then_inc(s_rank, 1)

            def spread_v(g, j):
                for b in range(GB):
                    rows = [d[:, bass.ds(g * GB + b, 1), :].rearrange("p o t -> p (o t)") for d in (dv_hi, dv_lo)]
                    ps = bank[2 * (j % 2) + b][:, 0:TP]
                    nc.tensor.matmul(ps, spread[:, j, :], rows[0], start=True, stop=False)
                    last = nc.tensor.matmul(ps, spread[:, j, :], rows[1], start=False, stop=True)
                last.then_inc(s_vb, 1)

            def project():
                for j in range(BPG):
                    nc.tensor.matmul(bank[6][:, j:j + 1], o_sq[:, j * P:(j + 1) * P], ones[:, 0:1], start=True, stop=True)
                for j in range(BPG):
                    last = nc.tensor.matmul(bank[7][:, j * D:(j + 1) * D], o_t[:, j * P:(j + 1) * P], gwo[:],
                                            start=True, stop=True)
                last.then_inc(s_att, 1)

            def attention(g, first, last):
                spread_v(g, 1)
                nc.tensor.matmul(bank[5][:], head_ones[:], q_t[:, bass.ds(g, 1), :].rearrange("p o t -> p (o t)"),
                                 start=True, stop=True).then_inc(s_qsum, 1)
                for j in range(DK):
                    if j + 2 < DK:
                        pe.wait_ge(s_scan, GB * (g * DK + j + 1))
                        spread_v(g, j + 2)
                    elif j + 2 == DK and not last:
                        pe.wait_ge(s_scan, GB * (g * DK + j + 1))
                        spread_v(g + 1, 0)
                    pe.wait_ge(s_qs, g * DK + j + 1)
                    if j == 0 and not first:
                        pe.wait_ge(s_ot, g)
                    nc.tensor.matmul(bank[4][:], gather[:, j, :], qstate[:, j % 2], start=(j == 0),
                                     stop=(j == DK - 1)).then_inc(s_red, 1)
                    if j == 1 and not first and not last:
                        pe.wait_ge(s_osq, g)
                        project()
                    if j == RANK_AT and first:
                        ranks()
                pe.wait_ge(s_scan, GB * (g + 1) * DK)

            pe.wait_ge(s_const, CONSTS)
            pe.wait_ge(s_q, G)
            pe.wait_ge(s_dvl, G)
            pe.wait_ge(s_spread, 1)
            pe.wait_ge(s_gwo, 1)
            pe.wait_ge(s_b1, 1)
            spread_v(0, 0)
            attention(0, True, False)
            pe.wait_ge(s_pos, 1)
            with pe.Fori(1, G - 1) as g:
                attention(g, False, False)
            pe.wait_ge(s_osq, G - 1)
            project()

            def turn(s, u):
                nc.tensor.transpose(bank[4 + u % 2][:, 0:P], xs[u][:, 0:D], ident[:]).then_inc(s_tr, 1)

            def layer1(t, u):
                pe.wait_ge(s_xst, t + 1)
                pe.wait_ge(s_w1, t + 1)
                for c in range(FC):
                    last = nc.tensor.matmul(bank[2 + u % 2][:, c * P:(c + 1) * P], w1_now[u % 2][:, c * P:(c + 1) * P],
                                            xs_t[u % 2][:], start=True, stop=True)
                last.then_inc(s_l1, 1)

            def layer2(t, u, e):
                pe.wait_ge(s_hg, t + 1)
                for c in range(FC):
                    last = nc.tensor.matmul(bank[6 + u % 2][:, 0:D], hg[u][:, c * P:(c + 1) * P],
                                            w2[:, bass.ds(e, 1), c * D:(c + 1) * D].rearrange("p o f -> p (o f)"),
                                            start=(c == 0), stop=(c == FC - 1))
                last.then_inc(s_l2, 1)

            def experts(t, n):
                regs = [pe.alloc_register(f"expert_{k}_{next(serial)}") for k in range(n)]
                pe.load(regs, own[0:1, bass.ds(t, n)])
                return [pe.snap(r, min_val=0, max_val=E - 1) for r in regs]

            pe.wait_ge(s_wexp, 48)
            pe.wait_ge(s_own, 1)
            pe.wait_ge(s_acc, G - 1)
            for t in range(2):
                pe.wait_ge(s_xs[t], 16)
                turn(t, t)
            layer1(0, 0)
            pe.wait_ge(s_xst, 1)
            pe.wait_ge(s_xs[2], 16)
            turn(2, 2)
            layer1(1, 1)

            def steps(i):
                ex = experts(RING * i, RING)
                for u in range(RING):
                    s = RING * i + LAG + u
                    a, b, c = (LAG + u) % RING, (LAG + u - 1) % RING, u
                    pe.wait_ge(s_xs[a], 16 * (i + (LAG + u) // RING + 1))
                    pe.wait_ge(s_xst, s - 1)
                    turn(s, a)
                    pe.wait_ge(s_hb, s - 2)
                    layer1(s - 1, b)
                    if not isinstance(s, int) or s > 4:
                        pe.wait_ge(s_yb, s - 4)
                    layer2(s - 3, c, ex[u])

            steps(0)
            with pe.Fori(1, ROUNDS) as i:
                steps(i)
            ex = experts(TILES - 3, 3)
            pe.wait_ge(s_hb, TILES - 2)
            layer1(TILES - 1, (TILES - 1) % RING)
            for t in range(TILES - 3, TILES):
                pe.wait_ge(s_yb, t - 1)
                layer2(t, t % RING, ex[t - TILES + 3])
            pe.wait_ge(s_yb, TILES)
            attention(G - 1, False, True)
            pe.wait_ge(s_osq, G)
            project()

        @block.vector
        def _(dve):
            chain = [0]

            def link(ins):
                chain[0] += 1
                ins.then_inc(s_dve, 1)
                dve.wait_ge(s_dve, chain[0])

            V = nc.vector

            def rsqrt(y, x, t):
                yield V.tensor_scalar(t.bitcast(I32), x.bitcast(I32), 1, None, ALU.logical_shift_right)
                yield V.tensor_scalar(y.bitcast(I32), t.bitcast(I32), -1.0, RSQRT_GUESS, ALU.mult, ALU.add)
                for _ in range(NEWTON):
                    yield V.tensor_tensor(t, y, y, ALU.mult)
                    yield V.scalar_tensor_tensor(out=t, in0=t, scalar=-0.5, in1=x, op0=ALU.mult, op1=ALU.mult)
                    yield V.scalar_tensor_tensor(out=y, in0=t, scalar=1.5, in1=y, op0=ALU.add, op1=ALU.mult)

            def layernorm(first, last):
                for g in range(first, last):
                    dve.wait_ge(s_x[g], 16)
                    for n in range(g * BPG, (g + 1) * BPG):
                        ins = V.bn_stats(stats[:, n, :], x_sb[:, n, :])
                ns = slice(first * BPG, last * BPG)
                link(ins)
                for n in range(first * BPG, last * BPG):
                    ins = V.bn_aggr(mean_var[:, n, :], stats[:, n, :])
                link(ins)
                link(V.tensor_scalar(var[:, ns], mean_var[:, ns, 1], LN_EPS, None, ALU.add))
                for ins in rsqrt(rstd[:, ns], var[:, ns], halves[:, ns]):
                    link(ins)
                for g in range(first, last):
                    for n in range(g * BPG, (g + 1) * BPG):
                        ins = V.tensor_scalar(xn[:, n, 0:D], x_sb[:, n, :], mean_var[:, n, 0:1], rstd[:, n:n + 1],
                                              ALU.subtract, ALU.mult)
                    ins.then_inc(s_xn, 1)

            dve.wait_ge(s_cent, 16)
            link(V.tensor_tensor(cent_sq[:], cent[:], cent[:], ALU.mult))
            link(V.tensor_reduce(cent_s[:, 0:1], cent_sq[:], AX.X, ALU.add))
            for ins in rsqrt(cent_s[:, 2:3], cent_s[:, 0:1], cent_s[:, 1:2]):
                link(ins)
            link(V.tensor_scalar(cent_s[:, 3:4], cent_s[:, 2:3], MAX_NORM, 1.0, ALU.mult, ALU.min))
            V.tensor_scalar(cent_p[:], cent[:], cent_s[:, 3:4], None, ALU.mult).then_inc(s_cp, 1)
            layernorm(0, 1)
            dve.wait_ge(s_cpe, 1)
            link(V.tensor_copy(cp_t[:], bank[6][:, 0:E]))
            V.tensor_tensor(cp_sq[:], cp_t[:], cp_t[:], ALU.mult).then_inc(s_cpt, 1)
            layernorm(1, G)
            for g in range(G):
                dve.wait_ge(s_sigq, g + 1)
                V.scalar_tensor_tensor(out=q_t[:, g, :], in0=bank[5][:], scalar=QSCALE, in1=sig_q[:, g % 2],
                                       op0=ALU.mult, op1=ALU.mult).then_inc(s_q, 1)
            dve.wait_ge(s_b1t, 1)
            V.tensor_copy(b1[:].rearrange("p e c -> p (e c)"), bank[6][:, 2 * E:2 * E + E * FC]).then_inc(s_b1, 1)
            dve.wait_ge(s_cpe, 2)
            link(V.tensor_scalar(c_n2[:], bank[6][:, E:2 * E], NORM_CAP, None, ALU.min))
            link(V.tensor_scalar(c_om[:], c_n2[:], -1.0, 1.0, ALU.mult, ALU.add))

            def tok(i):
                return r_tok[i][:].unsqueeze(2).to_broadcast([P, NB, E])

            def exp(a):
                return a[:].unsqueeze(1).to_broadcast([P, NB, E])

            def settled(ins):
                chain[0] += 1
                ins.then_inc(s_dve, 1)
                return chain[0]

            def routing():
                dve.wait_ge(s_rp, G)
                got = bank[7][:, 0:NB * 2 * E].rearrange("p (n c) -> p n c", c=2 * E)
                n = settled(V.tensor_copy(prod[:], got[:, :, 0:E + 1]))
                yield
                dve.wait_ge(s_dve, n)
                n = settled(V.tensor_copy(r_tok[0][:], prod[:, :, E]))
                yield
                dve.wait_ge(s_dve, n)
                for ins in rsqrt(r_tok[1][:], r_tok[0][:], r_tok[2][:]):
                    n = settled(ins)
                    yield
                    dve.wait_ge(s_dve, n)
                n = settled(V.tensor_scalar(r_tok[2][:], r_tok[1][:], MAX_NORM, 1.0, ALU.mult, ALU.min))
                yield
                dve.wait_ge(s_dve, n)
                V.tensor_tensor(r_big[0][:], prod[:, :, 0:E], tok(2), ALU.mult)
                n = settled(V.tensor_tensor(r_tok[3][:], r_tok[0][:], r_tok[2][:], ALU.mult))
                yield
                dve.wait_ge(s_dve, n)
                n = settled(V.tensor_tensor(r_tok[4][:], r_tok[3][:], r_tok[2][:], ALU.mult))
                yield
                dve.wait_ge(s_dve, n)
                n = settled(V.tensor_scalar(r_tok[5][:], r_tok[4][:], NORM_CAP, None, ALU.min))
                yield
                dve.wait_ge(s_dve, n)
                n = settled(V.scalar_tensor_tensor(out=r_big[1][:], in0=r_big[0][:], scalar=-2.0, in1=tok(5), op0=ALU.mult, op1=ALU.add))
                yield
                dve.wait_ge(s_dve, n)
                V.tensor_tensor(r_big[2][:], r_big[1][:], exp(c_n2), ALU.add)
                n = settled(V.tensor_scalar(r_tok[6][:], r_tok[5][:], -1.0, 1.0, ALU.mult, ALU.add))
                yield
                dve.wait_ge(s_dve, n)
                n = settled(V.tensor_tensor(r_big[3][:], tok(6), exp(c_om), ALU.mult))
                yield
                dve.wait_ge(s_dve, n)
                n = settled(V.tensor_scalar(r_big[4][:], r_big[3][:], BALL_EPS, None, ALU.add))
                yield
                dve.wait_ge(s_dve, n)
                V.tensor_scalar(r_big[1][:], r_big[2][:], 0.0, 2.0, ALU.max, ALU.mult)
                n = settled(V.reciprocal(r_big[5][:], r_big[4][:]))
                yield
                dve.wait_ge(s_dve, n)
                n = settled(V.tensor_tensor(r_big[6][:], r_big[1][:], r_big[5][:], ALU.mult))
                yield
                dve.wait_ge(s_dve, n)
                n = settled(V.tensor_scalar(r_big[0][:], r_big[6][:], 1.0, ARG_MIN, ALU.add, ALU.max))
                yield
                dve.wait_ge(s_dve, n)
                hot = (r_big[7], r_big[8])
                arg = r_big[0]
                for k in range(TOPK):
                    n = settled(V.tensor_reduce(m12[:, k, :], arg[:], AX.X, ALU.min))
                    yield
                    dve.wait_ge(s_dve, n)
                    n = settled(V.tensor_tensor(r_big[2][:], arg[:], m12[:, k, :].unsqueeze(2).to_broadcast([P, NB, E]), ALU.is_equal))
                    yield
                    dve.wait_ge(s_dve, n)
                    n = settled(V.scalar_tensor_tensor(out=r_big[3][:], in0=r_big[2][:], scalar=-float(E), in1=exp(iota_e8),
                                                op0=ALU.mult, op1=ALU.add))
                    yield
                    dve.wait_ge(s_dve, n)
                    n = settled(V.tensor_reduce(r_tok[7][:], r_big[3][:], AX.X, ALU.min))
                    yield
                    dve.wait_ge(s_dve, n)
                    n = settled(V.tensor_tensor(hot[k][:], exp(iota_e), tok(7), ALU.is_equal))
                    yield
                    dve.wait_ge(s_dve, n)
                    if k == 0:
                        n = settled(V.scalar_tensor_tensor(out=r_big[1][:], in0=hot[0][:], scalar=FAR, in1=arg[:], op0=ALU.mult, op1=ALU.add))
                        yield
                        dve.wait_ge(s_dve, n)
                        arg = r_big[1]
                V.tensor_tensor(r_big[9][:], hot[0][:], hot[1][:], ALU.add).then_inc(s_route, 1)
                n = settled(V.tensor_scalar(u_a[:], m12[:], 1.0, None, ALU.subtract))
                yield
                dve.wait_ge(s_dve, n)
                n = settled(V.scalar_tensor_tensor(out=u_b[:], in0=m12[:], scalar=1.0, in1=u_a[:], op0=ALU.add, op1=ALU.mult))
                yield
                dve.wait_ge(s_dve, n)
                for ins in rsqrt(u_a[:], u_b[:], u_c[:]):
                    n = settled(ins)
                    yield
                    dve.wait_ge(s_dve, n)
                n = settled(V.tensor_tensor(u_c[:], u_a[:], u_b[:], ALU.mult))
                yield
                dve.wait_ge(s_dve, n)
                n = settled(V.tensor_tensor(u_b[:], u_c[:], m12[:], ALU.add))
                yield
                dve.wait_ge(s_dve, n)
                n = settled(V.reciprocal(u_a[:, 1, :], u_b[:, 1, :]))
                yield
                dve.wait_ge(s_dve, n)
                n = settled(V.tensor_tensor(r_tok[0][:], u_b[:, 0, :], u_a[:, 1, :], ALU.mult))
                yield
                dve.wait_ge(s_dve, n)
                n = settled(V.tensor_scalar(r_tok[1][:], r_tok[0][:], 1.0, None, ALU.add))
                yield
                dve.wait_ge(s_dve, n)
                n = settled(V.reciprocal(weight[:, 0, :], r_tok[1][:]))
                yield
                dve.wait_ge(s_dve, n)
                n = settled(V.tensor_tensor(weight[:, 1, :], r_tok[0][:], weight[:, 0, :], ALU.mult))
                yield
                dve.wait_ge(s_dve, n)
                dve.wait_ge(s_rank, 1)
                rank = bank[6][:, 0:NB * E].rearrange("p (n e) -> p e n", e=E)
                total = bank[6][:, NB * E:2 * NB * E].rearrange("p (n e) -> p e n", e=E)
                n = settled(V.tensor_copy(tot[:], total))
                yield
                dve.wait_ge(s_dve, n)
                n = settled(V.tensor_tensor_scan(inc[:].rearrange("p e n -> p (e n)"), not_first[:].rearrange("p e n -> p (e n)"),
                                          tot[:].rearrange("p e n -> p (e n)"), 0.0, ALU.mult, ALU.add))
                yield
                dve.wait_ge(s_dve, n)
                V.tensor_tensor(exc[:], inc[:], tot[:], ALU.subtract)
                n = settled(V.tensor_scalar(cnt_i[:, 0, :], inc[:, :, NB - 1], float(P - 1), None, ALU.add))
                yield
                dve.wait_ge(s_dve, n)
                SH = P.bit_length() - 1
                n = settled(V.tensor_scalar(cnt_i[:, 1, :], cnt_i[:, 0, :], SH, SH, ALU.logical_shift_right, ALU.logical_shift_left))
                yield
                dve.wait_ge(s_dve, n)
                n = settled(V.tensor_copy(pad_f[:, 0, :], cnt_i[:, 1, :]))
                yield
                dve.wait_ge(s_dve, n)
                n = settled(V.tensor_tensor_scan(pad_f[:, 1, :], ones[:, 0:E], pad_f[:, 0, :], 0.0, ALU.mult, ALU.add))
                yield
                dve.wait_ge(s_dve, n)
                n = settled(V.tensor_tensor(pad_f[:, 2, :], pad_f[:, 1, :], pad_f[:, 0, :], ALU.subtract))
                yield
                dve.wait_ge(s_dve, n)
                n = settled(V.tensor_tensor(tot[:], exc[:], pad_f[:, 2, :].unsqueeze(2).to_broadcast([P, E, NB]), ALU.add))
                yield
                dve.wait_ge(s_dve, n)
                n = settled(V.tensor_tensor(inc[:], rank, tot[:], ALU.add))
                yield
                dve.wait_ge(s_dve, n)
                for k in range(TOPK):
                    n = settled(V.tensor_tensor(r_big[2][:], hot[k][:], inc[:].rearrange("p e n -> p n e"), ALU.mult))
                    yield
                    dve.wait_ge(s_dve, n)
                    n = settled(V.tensor_reduce(pos_f[:, k, :], r_big[2][:], AX.X, ALU.add))
                    yield
                    dve.wait_ge(s_dve, n)
                V.tensor_copy(pos[:], pos_f[:]).then_inc(s_pos, 1)
                n = settled(V.tensor_tensor(own_f[:], pad_f[0:1, 1, :].unsqueeze(1).to_broadcast([1, TILES, E]),
                                     tile_row[:].unsqueeze(2).to_broadcast([1, TILES, E]), ALU.is_le))
                yield
                dve.wait_ge(s_dve, n)
                n = settled(V.tensor_reduce(own_s[:, 0, :], own_f[:], AX.X, ALU.add))
                yield
                dve.wait_ge(s_dve, n)
                n = settled(V.tensor_scalar(own_s[:, 1, :], own_s[:, 0, :], float(E - 1), None, ALU.min))
                yield
                dve.wait_ge(s_dve, n)
                V.tensor_copy(own[:, 0:TILES], own_s[:, 1, :]).then_inc(s_own, 1)

            def scans(g, j):
                n = g * DK + j
                dve.wait_ge(s_vb, n + 1)
                if not isinstance(n, int) or n >= 4:
                    dve.wait_ge(s_qs, n - 3)
                for b in range(GB):
                    V.tensor_tensor_scan(state[:, j % 4, b, :], gate[:, bass.ds(g * GB + b, 1), :].rearrange("p o t -> p (o t)"),
                                         bank[2 * (j % 2) + b][:, 0:TP], 0.0, ALU.mult, ALU.add).then_inc(s_scan, 1)

            def times_q(g, j):
                n = g * DK + j
                dve.wait_ge(s_scan, GB * (n + 1))
                if not isinstance(n, int) or n >= 2:
                    dve.wait_ge(s_red, n - 1)
                V.tensor_tensor(qstate[:, j % 2].rearrange("p (b t) -> p b t", b=GB), state[:, j % 4, :, 1:T + 1],
                                q_t[:, bass.ds(g, 1), :].rearrange("p o (b t) -> p (o b) t", b=GB),
                                ALU.mult).then_inc(s_qs, 1)

            def finish(g):
                done = RMS_STEPS * g
                dve.wait_ge(s_att, g + 1)
                V.tensor_scalar(rms[:, 0, :], bank[6][:, 0:BPG], 1.0 / D, RMS_EPS, ALU.mult, ALU.add).then_inc(s_rms, 1)
                yield
                dve.wait_ge(s_rms, done + 1)
                for k, ins in enumerate(rsqrt(rms[:, 1, :], rms[:, 0, :], rms[:, 2, :])):
                    ins.then_inc(s_rms, 1)
                    yield
                    dve.wait_ge(s_rms, done + k + 2)
                for j in range(BPG):
                    n = bass.ds(g * BPG + j, 1)
                    ins = V.scalar_tensor_tensor(out=acc[:, n, :].rearrange("p o d -> p (o d)"), in0=bank[7][:, j * D:(j + 1) * D],
                                                 scalar=rms[:, 1, j:j + 1], in1=x_sb[:, n, :].rearrange("p o d -> p (o d)"),
                                                 op0=ALU.mult, op1=ALU.add)
                ins.then_inc(s_acc, 1)

            def attention(g, last, between, start, each):
                for j in range(DK):
                    if j + 1 < DK:
                        scans(g, j + 1)
                    elif not last:
                        scans(g + 1, 0)
                    if j >= start:
                        for _ in range(each):
                            next(between, None)
                    times_q(g, j)
                    if j >= start:
                        for _ in range(each):
                            next(between, None)
                    if j == 1:
                        dve.wait_ge(s_qsum, g + 1)
                        V.tensor_tensor(q_v[:].rearrange("p (b t) -> p b t", b=GB), bank[5][:].rearrange("p (b t) -> p b t", b=GB),
                                        v_t[:, bass.ds(g * GB, GB), 2:T + 2], ALU.mult).then_inc(s_qv, 1)
                for _ in between:
                    pass
                dve.wait_ge(s_red, (g + 1) * DK)
                dve.wait_ge(s_qv, g + 1)
                V.tensor_tensor(o_t[:], bank[4][:], q_v[:], ALU.add).then_inc(s_ot, 1)

            dve.wait_ge(s_gate, G)
            scans(0, 0)
            attention(0, False, routing(), 0, 3)
            with dve.Fori(1, G - 1) as g:
                attention(g, False, finish(g - 1), 2, 1)
            for _ in finish(G - 2):
                pass

            def take_weights(t, u, e):
                V.tensor_copy(w1_now[u % 2][:], w1[:, bass.ds(e, 1), :].rearrange("p o f -> p (o f)")).then_inc(s_w1, 1)

            def take_places(t, u):
                V.tensor_copy(place[u][:], xs[u][:, D:D + 1].bitcast(U32)).then_inc(s_place, 1)

            def bias1(t, u, e):
                dve.wait_ge(s_l1, t + 1)
                V.tensor_tensor(hb[u % 2][:].rearrange("p (c t) -> p c t", c=FC), bank[2 + u % 2][:].rearrange("p (c t) -> p c t", c=FC),
                                b1[:, bass.ds(e, 1), :].rearrange("p o c -> p (o c)").unsqueeze(2).to_broadcast([P, FC, P]),
                                ALU.add).then_inc(s_hb, 1)

            def bias2(t, u, e):
                dve.wait_ge(s_place, t + 1)
                V.tensor_copy(place_y[u][:], place[u][:])
                dve.wait_ge(s_l2, t + 1)
                V.tensor_tensor(yb[u][:], bank[6 + u % 2][:, 0:D], b2[:, bass.ds(e, 1), :].rearrange("p o f -> p (o f)"), ALU.add).then_inc(s_yb, 1)

            def experts(t, n):
                regs = [dve.alloc_register(f"expert_{k}_{next(serial)}") for k in range(n)]
                dve.load(regs, own[0:1, bass.ds(t, n)])
                return [dve.snap(r, min_val=0, max_val=E - 1) for r in regs]

            dve.wait_ge(s_wexp, 48)
            dve.wait_ge(s_own, 1)
            ex = experts(0, 3)
            take_weights(0, 0, ex[0])
            take_weights(1, 1, ex[1])
            for t in range(3):
                dve.wait_ge(s_xs[t], 16)
                take_places(t, t)
            bias1(0, 0, ex[0])
            take_weights(2, 2, ex[2])
            bias1(1, 1, ex[1])

            def steps(i):
                ex = experts(RING * i, RING + LAG)
                for u in range(RING):
                    s = RING * i + LAG + u
                    a, b, c = (LAG + u) % RING, (LAG + u - 1) % RING, u
                    dve.wait_ge(s_l1, s - 1)
                    take_weights(s, a, ex[u + LAG])
                    dve.wait_ge(s_hg, s - 2)
                    bias1(s - 1, b, ex[u + LAG - 1])
                    dve.wait_ge(s_xs[a], 16 * (i + (LAG + u) // RING + 1))
                    if not isinstance(s, int) or s > 3:
                        dve.wait_ge(s_yb, s - 3)
                    take_places(s, a)
                    if not isinstance(i, int):
                        dve.wait_ge(s_ys[c], 16 * i)
                    bias2(s - 3, c, ex[u])

            steps(0)
            with dve.Fori(1, ROUNDS) as i:
                steps(i)
            ex = experts(TILES - 3, 3)
            dve.wait_ge(s_hg, TILES - 2)
            bias1(TILES - 1, (TILES - 1) % RING, ex[2])
            for t in range(TILES - 3, TILES):
                dve.wait_ge(s_ys[t % RING], 16 * (t // RING))
                bias2(t, t % RING, ex[t - TILES + 3])
            attention(G - 1, True, iter(()), DK, 0)
            for _ in finish(G - 1):
                pass
            dve.wait_ge(s_acc, G)
            for g in range(G):
                dve.wait_ge(s_yg[g], 16 * TOPK)
                for k in range(TOPK):
                    for n in range(g * BPG, (g + 1) * BPG):
                        ins = V.scalar_tensor_tensor(out=acc[:, n, :], in0=y_rows[:, k, n, :], scalar=weight[:, k, n:n + 1],
                                                     in1=acc[:, n, :], op0=ALU.mult, op1=ALU.add)
                    if k + 1 < TOPK:
                        link(ins)
                ins.then_inc(s_fin, 1)


_INS = ["L0_attn_hidden_states", "L0_attn_Wq", "L0_attn_Wf", "L0_attn_Wi", "L0_attn_g_weight", "L0_attn_Wo",
        "L0_ffn_centroids", "L0_ffn_Wp", "L0_ffn_bp", "L0_ffn_W1", "L0_ffn_b1", "L0_ffn_W2", "L0_ffn_b2"]


def kernel(**inputs):
    import numpy as _np
    import concourse.bacc as _bacc
    from concourse import mybir as _mybir
    from concourse.bass_utils import run_bass_kernel_spmd as _run

    nc = _bacc.Bacc("TRN2", target_bir_lowering=False, num_devices=1)
    arrays, args = {}, []
    for name in _INS:
        a = _np.ascontiguousarray(inputs[name])
        arrays[f"in_{name}_dram"] = a
        args.append(nc.dram_tensor(f"in_{name}_dram", a.shape, _mybir.dt.from_np(a.dtype), kind="ExternalInput").ap())
    shape = inputs["L0_attn_hidden_states"].shape
    args.append(nc.dram_tensor("out_0_dram", shape, _mybir.dt.float32, kind="ExternalOutput").ap())
    gla_and_routed_experts(nc, *args)
    r = _run(nc, [arrays], core_ids=[0])
    return r.results[0]["out_0_dram"]
```

```python
from contextlib import ExitStack

import numpy as np
import concourse.bass as bass
from concourse import mybir

F32 = mybir.dt.float32
F32R = mybir.dt.float32r
I32 = mybir.dt.int32
U32 = mybir.dt.uint32
ALU = mybir.AluOpType
ACT = mybir.ActivationFunctionType
AX = mybir.AxisListType

P = 128


def gla_and_routed_experts(
    nc: bass.Bass,
    x_in: bass.AP,
    wq_in: bass.AP,
    wf_in: bass.AP,
    wi_in: bass.AP,
    gw_in: bass.AP,
    wo_in: bass.AP,
    cent_in: bass.AP,
    wp_in: bass.AP,
    bp_in: bass.AP,
    w1_in: bass.AP,
    b1_in: bass.AP,
    w2_in: bass.AP,
    b2_in: bass.AP,
    out: bass.AP,
):
    BATCH, T, D = x_in.shape
    H = 8
    DK = D // H
    E, _, F = w1_in.shape
    N = BATCH * T
    NB = N // P
    GB = 2
    G = BATCH // GB
    GT = GB * T
    BPG = GT // P
    TOPK = 2
    TILES = (N * TOPK + E * (P - 1)) // P
    FC = F // P
    RING = 4
    BANK = 512
    TP = T + 2
    LN_EPS = RMS_EPS = 1e-5
    MAX_NORM, BALL_EPS, NORM_CAP = 0.95, 1e-7, 0.99
    ARG_MIN = float(np.float32(1.0) + np.float32(BALL_EPS))
    FAR = 1e30
    RSQRT_GUESS = float(0x5F3759DF)
    NEWTON = 3
    RMS_STEPS = 3 + 3 * NEWTON
    QUERIES_AT = 3
    DIFFERENCES_AT = (1, 4, 7)
    ROUTING_EACH = 2
    RANK_AT = 9
    ON_POOL = (9, 11, 13)
    WARM = 20
    QSCALE = float(DK) ** -0.5
    assert D == P and GB == 2 and GT == BANK and F == BANK and TILES == 39 and DK * H == D

    ROWS_OUT = TOPK * N
    xs_dram = nc.dram_tensor("rows_by_expert", (TILES * P, D + 1), F32).ap()
    ys_dram = nc.dram_tensor("expert_rows_out", (ROWS_OUT, D), F32).ap()

    with ExitStack() as ctx:
        def sb(name, shape, dt=F32):
            return ctx.enter_context(nc.sbuf_tensor(name, shape, dt))

        def sem(name):
            return ctx.enter_context(nc.semaphore(name))

        pair = [ctx.enter_context(nc.psum_tensor(f"pair{i}", [P, GB, BANK], F32)) for i in range(2)]
        bank = [pair[i // 2][:, i % 2, :] for i in range(4)]
        bank += [ctx.enter_context(nc.psum_tensor(f"bank{i}", [P, BANK], F32)) for i in range(4, 8)]

        x_sb = sb("x_sb", [P, NB, D])
        xn = sb("xn", [P, NB, D + 1])
        xn_t = sb("xn_t", [P, G, GT])
        acc = x_sb
        stats = sb("stats", [P, NB, 6])
        mean_var = sb("mean_var", [P, NB, 2])
        var = sb("var", [P, NB])
        rstd = sb("rstd", [P, NB])
        halves = sb("halves", [P, NB])

        wq = sb("wq", [P, D])
        wf = sb("wf", [P, D])
        wi = sb("wi", [P, D])
        wp = sb("wp", [P, D])
        wo = sb("wo", [P, D])
        gwo = sb("gwo", [P, D])
        gw = sb("gw", [P, 1])
        bp = sb("bp", [P, 1])
        w1 = sb("w1", [P, E, F])
        w2 = sb("w2", [P, E, FC * D])
        b1_rows = sb("b1_rows", [E * FC, P])
        b1 = sb("b1", [P, E, FC])
        b2 = sb("b2", [P, E, D])

        ident = sb("ident", [P, P])
        ones = sb("ones", [P, P])
        before = sb("before", [P, P])
        head_ones = sb("head_ones", [P, D])
        spread = sb("spread", [P, DK, D], F32R)
        gather = sb("gather", [P, DK, D])
        no_rows = sb("no_rows", [P, D + 1])
        iota_e = sb("iota_e", [P, E])
        iota_e8 = sb("iota_e8", [P, E])
        tile_row = sb("tile_row", [1, TILES])
        not_first = sb("not_first", [P, E, NB])

        q_t = sb("q_t", [P, G, GT])
        gate = sb("gate", [P, BATCH, TP])
        v_t = sb("v_t", [P, BATCH, TP + 1])
        dv_f = sb("dv_f", [P, 2, GB, TP])
        dv_hi = sb("dv_hi", [P, BATCH, TP], F32R)
        dv_lo = sb("dv_lo", [P, BATCH, TP], F32R)
        sig_q = sb("sig_q", [P, 2, GT])
        state = sb("state", [P, 4, GB, TP])
        qstate = sb("qstate", [P, 2, GT])
        q_v = sb("q_v", [P, GT])
        o_t = sb("o_t", [P, GT])
        o_sq = sb("o_sq", [P, GT])
        norm2 = sb("norm2", [P, BPG])
        rms = sb("rms", [P, 3, BPG])

        xp_t = sb("xp_t", [P, 2, GT])
        xp_sq = sb("xp_sq", [P, NB, D])
        xnorm = sb("xnorm", [P, NB])
        cent = sb("cent", [E, D])
        cent_sq = sb("cent_sq", [E, D])
        cent_p = sb("cent_p", [E, D])
        cent_s = sb("cent_s", [E, 4])
        cp_t = sb("cp_t", [P, E])
        cp_sq = sb("cp_sq", [P, E])
        c_n2 = sb("c_n2", [P, E])
        c_om = sb("c_om", [P, E])
        prod = sb("prod", [P, NB, E])
        r_tok = [sb(f"r_tok{i}", [P, NB]) for i in range(8)]
        r_big = [sb(f"r_big{i}", [P, NB, E]) for i in range(10)]
        m12 = sb("m12", [P, TOPK, NB])
        u_a = sb("u_a", [P, TOPK, NB])
        u_b = sb("u_b", [P, TOPK, NB])
        u_c = sb("u_c", [P, TOPK, NB])
        weight = sb("weight", [P, TOPK, NB])
        tot = sb("tot", [P, E, NB])
        inc = sb("inc", [P, E, NB])
        exc = sb("exc", [P, E, NB])
        cnt_i = sb("cnt_i", [P, 2, E], I32)
        pad_f = sb("pad_f", [P, 3, E])
        pos_f = sb("pos_f", [P, TOPK, NB])
        pos = sb("pos", [P, TOPK, NB], U32)
        own_f = sb("own_f", [1, TILES, E])
        own_s = sb("own_s", [1, TILES])
        own = sb("own", [1, TILES + 1], I32)

        xs = [sb(f"xs{i}", [P, D + 1]) for i in range(RING)]
        place = [sb(f"place{i}", [P, 1], U32) for i in range(RING)]
        place_y = [sb(f"place_y{i}", [P, 1], U32) for i in range(RING)]
        w1_now = [sb(f"w1_now{i}", [P, F]) for i in range(2)]
        xs_t = [sb(f"xs_t{i}", [P, P]) for i in range(2)]
        hg = [xn_t[:, i, :] for i in range(RING)]
        hb = [sb(f"hb{i}", [P, F]) for i in range(2)]
        yb = [sb(f"yb{i}", [P, D]) for i in range(RING)]
        y_rows = sb("y_rows", [P, TOPK, NB, D])
        spread_f = y_rows[:, 0, :, :]

        s_x = [sem(f"s_x{g}") for g in range(G)]
        s_wproj = sem("s_wproj")
        s_wexp = sem("s_wexp")
        s_wo = sem("s_wo")
        s_cent = sem("s_cent")
        s_const = sem("s_const")
        s_zero = sem("s_zero")
        s_zfill = sem("s_zfill")
        s_dve = sem("s_dve")
        s_xn = sem("s_xn")
        s_xtp = sem("s_xtp")
        s_xnt = sem("s_xnt")
        s_pp = sem("s_pp")
        s_fp = sem("s_fp")
        s_ip = sem("s_ip")
        s_qp = sem("s_qp")
        s_xp = sem("s_xp")
        s_xpt = sem("s_xpt")
        s_xnorm = sem("s_xnorm")
        s_rp = sem("s_rp")
        s_gate = sem("s_gate")
        s_v = sem("s_v")
        s_sigq = sem("s_sigq")
        s_q = sem("s_q")
        s_dvf = sem("s_dvf")
        s_dvh = sem("s_dvh")
        s_dvl = sem("s_dvl")
        s_gwo = sem("s_gwo")
        s_cp = sem("s_cp")
        s_cpt = sem("s_cpt")
        s_cpe = sem("s_cpe")
        s_route = sem("s_route")
        s_rank = sem("s_rank")
        s_pos = sem("s_pos")
        s_ended = sem("s_ended")
        s_own = sem("s_own")
        s_sent = sem("s_sent")
        s_vb = sem("s_vb")
        s_again = sem("s_again")
        s_scan = sem("s_scan")
        s_qs = sem("s_qs")
        s_qs_pool = sem("s_qs_pool")
        s_red = sem("s_red")
        s_qsum = sem("s_qsum")
        s_qv = sem("s_qv")
        s_ot = sem("s_ot")
        s_turned = sem("s_turned")
        s_ms = sem("s_ms")
        s_att = sem("s_att")
        s_rms = sem("s_rms")
        s_acc = sem("s_acc")
        s_xs = [sem(f"s_xs{i}") for i in range(RING)]
        s_place = sem("s_place")
        s_w1 = sem("s_w1")
        s_b1t = sem("s_b1t")
        s_b1 = sem("s_b1")
        s_b1in = sem("s_b1in")
        s_ids = sem("s_ids")
        s_tr = sem("s_tr")
        s_xst = sem("s_xst")
        s_l1 = sem("s_l1")
        s_hb = sem("s_hb")
        s_hg = sem("s_hg")
        s_l2 = sem("s_l2")
        s_yb = sem("s_yb")
        s_ys = [sem(f"s_ys{i}") for i in range(RING)]
        s_yg = [sem(f"s_yg{g}") for g in range(G)]
        s_ysc = sem("s_ysc")
        s_ysum = sem("s_ysum")
        s_fin = sem("s_fin")
        s_half = sem("s_half")
        s_out = sem("s_out")

        x_rows = x_in.rearrange("b t d -> (b t) d").rearrange("(n p) d -> p n d", p=P)
        out_rows = out.rearrange("b t d -> (b t) d").rearrange("(n p) d -> p n d", p=P)

        LAG = 3
        ROUNDS = (TILES - LAG) // RING
        assert ROUNDS * RING + LAG == TILES

        def multiplied(n):
            if isinstance(n, int) and n < DK:
                if n in ON_POOL:
                    return s_qs_pool, ON_POOL.index(n) + 1
                return s_qs, n + 1 - len([m for m in ON_POOL if m < n])
            return s_qs, n + 1 - len(ON_POOL)

        serial = iter(range(1 << 20))
        block = ctx.enter_context(nc.Block())

        @block.sync
        def _(sp):
            for g in range(G):
                sp.dma_start(x_sb[:, g * BPG:(g + 1) * BPG, :], x_rows[:, g * BPG:(g + 1) * BPG, :]).then_inc(s_x[g], 16)
                if g == 0:
                    sp.dma_start(cent[:], cent_in).then_inc(s_cent, 16)
            sp.dma_start(b1_rows[:], b1_in.rearrange("e (c p) -> (e c) p", p=P)).then_inc(s_b1in, 16)
            sp.wait_ge(s_zero, 1)
            sp.dma_start(xs_dram.rearrange("(n p) d -> p n d", p=P),
                         no_rows[:].unsqueeze(1).to_broadcast([P, TILES, D + 1])).then_inc(s_zfill, 16)
            sp.dma_start(wo[:], wo_in).then_inc(s_wo, 16)
            sp.dma_start(gw[:], gw_in.rearrange("(p o) -> p o", o=1)).then_inc(s_wo, 16)
            sp.dma_start(w1[:], w1_in.rearrange("e d f -> d e f")).then_inc(s_wexp, 16)
            sp.dma_start(w2[:].rearrange("p e (c d) -> p e c d", c=FC),
                         w2_in.rearrange("e (c p) d -> p e c d", p=P)).then_inc(s_wexp, 16)
            sp.dma_start(b2[:].rearrange("p e f -> p (e f)"),
                         b2_in.rearrange("e f -> (e f)").partition_broadcast(P)).then_inc(s_wexp, 16)

            def load_rows(t, u):
                sp.dma_start(xs[u][:], xs_dram[bass.ds(t * P, P), :]).then_inc(s_xs[u], 16)

            sp.wait_ge(s_sent, 16 * TOPK * NB)
            for t in range(RING):
                load_rows(t, t)
            with sp.Fori(1, ROUNDS) as i:
                for u in range(RING):
                    t = RING * i + u
                    sp.wait_ge(s_tr, t - RING + 1)
                    sp.wait_ge(s_place, t - RING + 1)
                    load_rows(t, u)
            for t in range(RING * ROUNDS, TILES):
                sp.wait_ge(s_tr, t - RING + 1)
                sp.wait_ge(s_place, t - RING + 1)
                load_rows(t, t % RING)
            for u in range(RING):
                sp.wait_ge(s_ys[u], 16 * len(range(u, TILES, RING)))
            ys_rows = ys_dram.rearrange("(k n p) d -> p k n d", k=TOPK, p=P)
            for g in range(G):
                for k in range(TOPK):
                    sp.dma_start(y_rows[:, k, g * BPG:(g + 1) * BPG, :], ys_rows[:, k, g * BPG:(g + 1) * BPG, :]).then_inc(s_yg[g], 16)
            def store(first, last):
                sp.dma_start(out_rows[:, first:last, :], acc[:, first:last, :]).then_inc(s_out, 16)

            for g in range(G - 1):
                sp.wait_ge(s_fin, g + 1)
                store(g * BPG, (g + 1) * BPG)
            sp.wait_ge(s_half, 1)
            store((G - 1) * BPG, NB - BPG // 2)
            sp.wait_ge(s_acc, G)
            store(NB - BPG // 2, NB)
            sp.wait_ge(s_out, 16 * (G + 1))

        @block.gpsimd
        def _(pool):
            step = [0]

            def link(ins):
                step[0] += 1
                ins.then_inc(s_const, 1)
                pool.wait_ge(s_const, step[0])

            nc.gpsimd.memset(ones[:], 1.0).then_inc(s_const, 1)
            step[0] += 1
            link(nc.gpsimd.memset(ident[:], 0.0))
            link(nc.gpsimd.affine_select(out=ident[:], in_=ident[:], compare_op=ALU.not_equal, fill=1.0,
                                         base=0, pattern=[[-1, P]], channel_multiplier=1))
            link(nc.gpsimd.memset(v_t[:, :, 0:1], 0.0))
            link(nc.gpsimd.memset(v_t[:, :, T + 1:TP + 1], 0.0))
            link(nc.gpsimd.memset(gate[:, :, 0:1], 0.0))
            link(nc.gpsimd.memset(gate[:, :, T + 1:TP], 0.0))
            link(nc.gpsimd.memset(no_rows[:, 0:D], 0.0))
            nc.gpsimd.memset(no_rows[:, D:D + 1].bitcast(I32), ROWS_OUT).then_inc(s_zero, 1)
            link(nc.gpsimd.affine_select(out=before[:], in_=ones[:], compare_op=ALU.is_gt, fill=0.0,
                                         base=0, pattern=[[1, P]], channel_multiplier=-1))
            link(nc.gpsimd.iota(iota_e[:], [[1, E]], base=0, channel_multiplier=0, allow_small_or_imprecise_dtypes=True))
            link(nc.gpsimd.iota(iota_e8[:], [[1, E]], base=E, channel_multiplier=0, allow_small_or_imprecise_dtypes=True))
            link(nc.gpsimd.iota(tile_row[:], [[P, TILES]], base=0, channel_multiplier=0, allow_small_or_imprecise_dtypes=True))
            link(nc.gpsimd.memset(not_first[:], 1.0))
            link(nc.gpsimd.memset(not_first[:, :, 0], 0.0))
            ho = head_ones[:].rearrange("p (h d) -> p h d", h=H)
            link(nc.gpsimd.affine_select(out=ho, in_=ones[:].rearrange("p (h d) -> p h d", h=H), compare_op=ALU.is_ge,
                                         fill=0.0, base=0, pattern=[[-DK, H], [0, DK]], channel_multiplier=1))
            link(nc.gpsimd.affine_select(out=ho, in_=ho, compare_op=ALU.is_ge,
                                         fill=0.0, base=DK - 1, pattern=[[DK, H], [0, DK]], channel_multiplier=-1))
            link(nc.gpsimd.affine_select(out=gather[:].rearrange("p j (h d) -> p j h d", h=H),
                                         in_=ho.unsqueeze(1).to_broadcast([P, DK, H, DK]),
                                         compare_op=ALU.is_equal, fill=0.0, base=0,
                                         pattern=[[1, DK], [0, H], [-1, DK]], channel_multiplier=0))
            link(nc.gpsimd.memset(spread_f, 0.0))
            link(nc.gpsimd.affine_select(out=spread[:].rearrange("p j (h d) -> p j h d", h=H),
                                         in_=spread_f.rearrange("p j (h d) -> p j h d", h=H),
                                         compare_op=ALU.not_equal, fill=1.0, base=0,
                                         pattern=[[-1, DK], [-DK, H], [0, DK]], channel_multiplier=1))
            def differences(g):
                bs = slice(g * GB, (g + 1) * GB)
                pool.wait_ge(s_v, g + 1)
                nc.gpsimd.tensor_tensor(dv_f[:, g % 2], v_t[:, bs, 0:TP], v_t[:, bs, 1:TP + 1], ALU.subtract).then_inc(s_dvf, 1)
                pool.wait_ge(s_dvf, g + 1)
                pool.wait_ge(s_dvh, g + 1)
                nc.gpsimd.tensor_tensor(dv_lo[:, bs, :], dv_f[:, g % 2], dv_hi[:, bs, :].bitcast(F32), ALU.subtract).then_inc(s_dvl, 1)

            differences(0)
            for j in range(DK):
                if j in ON_POOL:
                    pool.wait_ge(s_q, 1)
                    pool.wait_ge(s_scan, j + 1)
                    pool.wait_ge(s_red, j - 1)
                    nc.gpsimd.tensor_tensor(qstate[:, j % 2].rearrange("p (b t) -> p b t", b=GB), state[:, j % 4, :, 1:T + 1],
                                            q_t[:, 0, :].rearrange("p (b t) -> p b t", b=GB), ALU.mult).then_inc(s_qs_pool, 1)
                if j in DIFFERENCES_AT:
                    differences(DIFFERENCES_AT.index(j) + 1)
            pool.wait_ge(s_xn, G)
            for k in range(TOPK):
                if k > 0:
                    pool.wait_ge(s_sent, 16 * k * NB)
                nc.gpsimd.iota(xn[:, :, D].bitcast(I32), [[P, NB]], base=k * N, channel_multiplier=1).then_inc(s_ids, 1)
                pool.wait_ge(s_ids, k + 1)
                if k == 0:
                    pool.wait_ge(s_pos, 1)
                    pool.wait_ge(s_zfill, 16)
                for n in range(NB):
                    nc.gpsimd.indirect_dma_start(
                        out=xs_dram, out_offset=bass.IndirectOffsetOnAxis(ap=pos[:, k, n:n + 1], axis=0),
                        in_=xn[:, n, :], in_offset=None).then_inc(s_sent, 16)

            pool.wait_ge(s_ended, 1)
            half = E // 2
            while half:
                link(nc.gpsimd.tensor_tensor(own_f[:, :, 0:half], own_f[:, :, 0:half], own_f[:, :, half:2 * half], ALU.add))
                half //= 2
            link(nc.gpsimd.tensor_scalar(own_s[:], own_f[:, :, 0], float(E - 1), None, ALU.min))
            nc.gpsimd.tensor_copy(own[:, 0:TILES], own_s[:]).then_inc(s_own, 1)

            last_row = pool.alloc_register("last_row")
            limit = pool.alloc_register("limit")
            pool.reg_mov(last_row, ROWS_OUT - 1)

            def return_rows(t, u):
                pool.wait_ge(s_yb, t + 1)
                pool.reg_add(limit, last_row, 0)
                nc.gpsimd.indirect_dma_start(
                    out=ys_dram, out_offset=bass.IndirectOffsetOnAxis(ap=place_y[u][:, 0:1], axis=0),
                    in_=yb[u][:], in_offset=None, bounds_check=pool.snap(limit, min_val=0, max_val=ROWS_OUT - 1), oob_is_err=False).then_inc(s_ys[u], 16)

            with pool.Fori(0, ROUNDS) as i:
                for u in range(RING):
                    return_rows(RING * i + u, u)
            for t in range(RING * ROUNDS, TILES):
                return_rows(t, t % RING)
            pool.wait_ge(s_acc, G - 1)
            for g in range(G):
                ns = slice(g * BPG, (g + 1) * BPG)
                pool.wait_ge(s_ysc, g + 1)
                nc.gpsimd.tensor_tensor(y_rows[:, 0, ns, :], y_rows[:, 0, ns, :], y_rows[:, 1, ns, :], ALU.add).then_inc(s_ysum, 1)
                pool.wait_ge(s_ysum, g + 1)
                nc.gpsimd.tensor_tensor(acc[:, ns, :], acc[:, ns, :], y_rows[:, 0, ns, :], ALU.add).then_inc(s_fin, 1)

        IDENT, EDGES, CONSTS = 3, 7, 19
        TURN_BANK = (0, 1, 2, 3)
        PP_BANK = (6, 4, 6, 4)
        I_F_Q_BANKS = ((3, 4, 5),) + ((6, 6, 6),) * (G - 1)

        @block.scalar
        def _(act):
            act.dma_start(wi[:], wi_in).then_inc(s_wproj, 16)
            act.dma_start(wf[:], wf_in).then_inc(s_wproj, 16)
            act.dma_start(wq[:], wq_in).then_inc(s_wproj, 16)
            act.dma_start(wp[:], wp_in).then_inc(s_wproj, 16)
            act.dma_start(bp[:], bp_in.rearrange("(p o) -> p o", o=1)).then_inc(s_wproj, 16)

            def channel_major(g):
                act.wait_ge(s_xtp, g + 1)
                nc.scalar.copy(xn_t[:, g, :], bank[TURN_BANK[g]][:]).then_inc(s_xnt, 1)

            def routing_projection(g):
                act.wait_ge(s_wproj, 16 * 5)
                act.wait_ge(s_pp, g + 1)
                if g >= 2:
                    act.wait_ge(s_rp, g - 1)
                nc.scalar.activation(xp_t[:, g % 2], bank[PP_BANK[g]][:], ACT.Identity, bias=bp[:, 0:1]).then_inc(s_xp, 1)

            def token_norms(g):
                act.wait_ge(s_xpt, g + 1)
                for j in range(BPG):
                    n = g * BPG + j
                    last = nc.scalar.activation(xp_sq[:, n, :], bank[5][:, j * D:(j + 1) * D], ACT.Square, accum_out=xnorm[:, n:n + 1])
                last.then_inc(s_xnorm, 1)

            def attention_projections(g):
                bs = slice(g * GB, (g + 1) * GB)
                b_i, b_f, b_q = I_F_Q_BANKS[g]
                act.wait_ge(s_ip, g + 1)
                if g == 0:
                    act.wait_ge(s_const, EDGES)
                nc.scalar.copy(v_t[:, bs, 1:T + 1], bank[b_i][:].rearrange("p (b t) -> p b t", b=GB)).then_inc(s_v, 1)
                act.wait_ge(s_fp, g + 1)
                nc.scalar.activation(gate[:, bs, 1:T + 1], bank[b_f][:].rearrange("p (b t) -> p b t", b=GB),
                                     ACT.Sigmoid).then_inc(s_gate, 1)
                act.wait_ge(s_dvf, g + 1)
                nc.scalar.copy(dv_hi[:, bs, :], dv_f[:, g % 2]).then_inc(s_dvh, 1)
                act.wait_ge(s_qp, g + 1)
                if g >= 2:
                    act.wait_ge(s_q, g - 1)
                nc.scalar.activation(sig_q[:, g % 2], bank[b_q][:], ACT.Sigmoid).then_inc(s_sigq, 1)

            channel_major(0)
            attention_projections(0)
            routing_projection(0)
            channel_major(1)
            channel_major(2)
            routing_projection(1)
            token_norms(0)
            channel_major(3)
            routing_projection(2)
            token_norms(1)
            routing_projection(3)
            token_norms(2)
            token_norms(3)
            act.wait_ge(s_wo, 32)
            nc.scalar.activation(gwo[:], wo[:], ACT.Copy, scale=gw[:, 0:1]).then_inc(s_gwo, 1)

            def attention(g):
                act.wait_ge(s_turned, g + 1)
                for j in range(BPG):
                    last = nc.scalar.activation(o_sq[:, j * D:(j + 1) * D], bank[6][:, j * D:(j + 1) * D], ACT.Square,
                                                accum_out=norm2[:, j:j + 1])
                last.then_inc(s_ms, 1)

            def turn(s, u):
                act.wait_ge(s_tr, s + 1)
                nc.scalar.copy(xs_t[u % 2][:], bank[5 - u % 2][:, 0:P]).then_inc(s_xst, 1)

            def gelu(t, u):
                act.wait_ge(s_hb, t + 1)
                nc.scalar.activation(hg[u], hb[u % 2][:], ACT.Gelu).then_inc(s_hg, 1)

            for g in range(1, G):
                attention_projections(g)
            with act.Fori(1, G - 1) as g:
                attention(g - 1)
            turn(0, 0)
            turn(1, 1)
            gelu(0, 0)
            act.wait_ge(s_l1, 1)
            turn(2, 2)
            attention(G - 2)
            gelu(1, 1)

            def steps(i):
                for u in range(RING):
                    s = RING * i + LAG + u
                    act.wait_ge(s_l1, s - 1)
                    turn(s, (LAG + u) % RING)
                    if not isinstance(s, int) or s > 4:
                        act.wait_ge(s_l2, s - 4)
                    gelu(s - 1, (LAG + u - 1) % RING)

            steps(0)
            with act.Fori(1, ROUNDS) as i:
                steps(i)
            act.wait_ge(s_l2, TILES - 4)
            gelu(TILES - 1, (TILES - 1) % RING)
            for g in range(G):
                act.wait_ge(s_yg[g], 16 * TOPK)
                for k in range(TOPK):
                    for n in range(g * BPG, (g + 1) * BPG):
                        last = nc.scalar.activation(y_rows[:, k, n, :], y_rows[:, k, n, :], ACT.Copy, scale=weight[:, k, n:n + 1])
                last.then_inc(s_ysc, 1)
            attention(G - 1)

        @block.tensor
        def _(pe):
            pe.wait_ge(s_const, 1)
            for _ in range(WARM):
                nc.tensor.matmul(bank[5][:, 0:P], ones[:], ones[:], start=True, stop=True)
            pe.wait_ge(s_const, IDENT)

            def turn_group(g):
                pe.wait_ge(s_xn, g + 1)
                for j in range(BPG):
                    last = nc.tensor.transpose(bank[TURN_BANK[g]][:, j * P:(j + 1) * P], xn[:, g * BPG + j, 0:D], ident[:])
                last.then_inc(s_xtp, 1)

            def distances(g):
                pe.wait_ge(s_xp, g + 1)
                if g == 0:
                    pe.wait_ge(s_q, 1)
                else:
                    pe.wait_ge(s_xnorm, g)
                for j in range(BPG):
                    last = nc.tensor.transpose(bank[5][:, j * P:(j + 1) * P], xp_t[:, g % 2, j * P:(j + 1) * P], ident[:])
                last.then_inc(s_xpt, 1)
                for j in range(BPG):
                    c = (g * BPG + j) * E
                    last = nc.tensor.matmul(bank[7][:, c:c + E], xp_t[:, g % 2, j * P:(j + 1) * P], cp_t[:], start=True, stop=True)
                last.then_inc(s_rp, 1)

            turn_group(0)
            pe.wait_ge(s_cp, 1)
            nc.tensor.transpose(bank[7][:, 0:E], cent_p[:], ident[0:E, 0:E]).then_inc(s_cpe, 1)
            pe.wait_ge(s_cpt, 1)
            nc.tensor.matmul(bank[7][:, E:2 * E], ones[:], cp_sq[:], start=True, stop=True).then_inc(s_cpe, 1)
            pe.wait_ge(s_b1in, 16)
            nc.tensor.transpose(bank[7][:, 2 * E:2 * E + E * FC], b1_rows[:], ident[0:E * FC, 0:E * FC]).then_inc(s_b1t, 1)
            pe.wait_ge(s_wproj, 16 * 5)
            pe.wait_ge(s_xnt, 1)
            for w, b, done in zip((wi, wf, wq), I_F_Q_BANKS[0], (s_ip, s_fp, s_qp)):
                nc.tensor.matmul(bank[b][:], w[:], xn_t[:, 0, :], start=True, stop=True).then_inc(done, 1)

            def routing_product(g):
                pe.wait_ge(s_xnt, g + 1)
                nc.tensor.matmul(bank[PP_BANK[g]][:], wp[:], xn_t[:, g, :], start=True, stop=True).then_inc(s_pp, 1)

            routing_product(0)
            turn_group(1)
            turn_group(2)
            pe.wait_ge(s_v, 1)
            routing_product(1)
            pe.wait_ge(s_b1, 1)
            distances(0)
            pe.wait_ge(s_gate, 1)
            turn_group(3)
            routing_product(2)
            distances(1)
            routing_product(3)

            def projections():
                for g in range(1, G):
                    for w, b, done, used, n in zip((wi, wf, wq), I_F_Q_BANKS[g], (s_ip, s_fp, s_qp), (s_q, s_v, s_gate), (g, g + 1, g + 1)):
                        pe.wait_ge(used, n)
                        nc.tensor.matmul(bank[b][:], w[:], xn_t[:, g, :], start=True, stop=True).then_inc(done, 1)
                        yield

            def ranks():
                pe.wait_ge(s_route, 1)
                pe.wait_ge(s_qv, 1)
                chosen = r_big[9][:].rearrange("p n e -> p (n e)")
                nc.tensor.matmul(bank[5][:, 0:NB * E], before[:], chosen, start=True, stop=True)
                nc.tensor.matmul(bank[5][:, NB * E:2 * NB * E], ones[:], chosen, start=True, stop=True).then_inc(s_rank, 1)

            def spread_v(g, j, done=s_vb):
                for b in range(GB):
                    rows = [d[:, bass.ds(g * GB + b, 1), :].rearrange("p o t -> p (o t)") for d in (dv_hi, dv_lo)]
                    ps = bank[2 * (j % 2) + b][:, BANK - TP:BANK] if b == 0 else bank[2 * (j % 2) + b][:, 0:TP]
                    nc.tensor.matmul(ps, spread[:, j, :], rows[0], start=True, stop=False)
                    last = nc.tensor.matmul(ps, spread[:, j, :], rows[1], start=False, stop=True)
                last.then_inc(done, 1)

            def project():
                for j in range(BPG):
                    last = nc.tensor.transpose(bank[6][:, j * D:(j + 1) * D], o_t[:, j * P:(j + 1) * P], ident[:])
                last.then_inc(s_turned, 1)
                for j in range(BPG):
                    last = nc.tensor.matmul(bank[7][:, j * D:(j + 1) * D], o_t[:, j * P:(j + 1) * P], gwo[:],
                                            start=True, stop=True)
                last.then_inc(s_att, 1)

            later = projections()

            def attention(g, first, last):
                def sum_q():
                    nc.tensor.matmul(bank[5][:], head_ones[:], q_t[:, bass.ds(g, 1), :].rearrange("p o t -> p (o t)"),
                                     start=True, stop=True).then_inc(s_qsum, 1)

                if not first:
                    sum_q()
                for j in range(DK):
                    if j + 3 < DK or not last:
                        if first and j + 3 == DK:
                            pe.wait_ge(s_dvl, G)
                        pe.wait_ge(s_scan, g * DK + j + 2)
                        if j + 3 < DK:
                            spread_v(g, j + 3)
                        else:
                            spread_v(g + 1, j + 3 - DK)
                    pe.wait_ge(*multiplied(g * DK + j))
                    if j == 0 and not first:
                        pe.wait_ge(s_ot, g)
                    nc.tensor.matmul(bank[4][:], gather[:, j, :], qstate[:, j % 2], start=(j == 0),
                                     stop=(j == DK - 1)).then_inc(s_red, 1)
                    if j == 2 and not first and not last:
                        pe.wait_ge(s_ot, g)
                        project()
                    if first and j == 0:
                        pe.wait_ge(s_xnorm, G)
                        sum_q()
                    if first:
                        next(later, None)
                    if j == RANK_AT and first:
                        ranks()
            pe.wait_ge(s_const, CONSTS)
            pe.wait_ge(s_dvl, 1)
            spread_v(0, 0)
            distances(2)
            pe.wait_ge(s_xnt, G)
            spread_v(0, 1)
            distances(3)
            pe.wait_ge(s_scan, 1)
            spread_v(0, 2)
            attention(0, True, False)
            pe.wait_ge(s_pos, 1)
            pe.wait_ge(s_q, G)
            pe.wait_ge(s_gwo, 1)
            with pe.Fori(1, G - 1) as g:
                attention(g, False, False)

            def turn(s, u):
                nc.tensor.transpose(bank[5 - u % 2][:, 0:P], xs[u][:, 0:D], ident[:]).then_inc(s_tr, 1)

            def layer1(t, u):
                pe.wait_ge(s_xst, t + 1)
                pe.wait_ge(s_w1, t + 1)
                for c in range(FC):
                    last = nc.tensor.matmul(bank[2 + u % 2][:, c * P:(c + 1) * P], w1_now[u % 2][:, c * P:(c + 1) * P],
                                            xs_t[u % 2][:], start=True, stop=True)
                last.then_inc(s_l1, 1)

            def layer2(t, u, e):
                pe.wait_ge(s_hg, t + 1)
                for c in range(FC):
                    last = nc.tensor.matmul(bank[u % 2][:, 0:D], hg[u][:, c * P:(c + 1) * P],
                                            w2[:, bass.ds(e, 1), c * D:(c + 1) * D].rearrange("p o f -> p (o f)"),
                                            start=(c == 0), stop=(c == FC - 1))
                last.then_inc(s_l2, 1)

            def experts(t, n):
                regs = [pe.alloc_register(f"expert_{k}_{next(serial)}") for k in range(n)]
                pe.load(regs, own[0:1, bass.ds(t, n)])
                return [pe.snap(r, min_val=0, max_val=E - 1) for r in regs]

            pe.wait_ge(s_wexp, 48)
            pe.wait_ge(s_own, 1)
            pe.wait_ge(s_xs[0], 16)
            turn(0, 0)
            pe.wait_ge(s_ot, G - 1)
            pe.wait_ge(s_xs[1], 16)
            turn(1, 1)
            layer1(0, 0)
            pe.wait_ge(s_xst, 1)
            pe.wait_ge(s_xs[2], 16)
            turn(2, 2)
            layer1(1, 1)
            project()

            def steps(i):
                ex = experts(RING * i, RING)
                for u in range(RING):
                    s = RING * i + LAG + u
                    a, b, c = (LAG + u) % RING, (LAG + u - 1) % RING, u
                    pe.wait_ge(s_xs[a], 16 * (i + (LAG + u) // RING + 1))
                    pe.wait_ge(s_xst, s - 1)
                    turn(s, a)
                    pe.wait_ge(s_hb, s - 2)
                    layer1(s - 1, b)
                    if not isinstance(s, int) or s > 4:
                        pe.wait_ge(s_yb, s - 4)
                    layer2(s - 3, c, ex[u])

            steps(0)
            with pe.Fori(1, ROUNDS) as i:
                steps(i)
            ex = experts(TILES - 3, 3)
            pe.wait_ge(s_hb, TILES - 2)
            layer1(TILES - 1, (TILES - 1) % RING)
            for t in range(TILES - 3, TILES):
                pe.wait_ge(s_yb, t - 1)
                layer2(t, t % RING, ex[t - TILES + 3])
            pe.wait_ge(s_yb, TILES)
            pe.wait_ge(s_acc, G - 1)
            spread_v(G - 1, 1, s_again)
            spread_v(G - 1, 2, s_again)
            attention(G - 1, False, True)
            pe.wait_ge(s_ot, G)
            project()

        @block.vector
        def _(dve):
            chain = [0]

            def link(ins):
                chain[0] += 1
                ins.then_inc(s_dve, 1)
                dve.wait_ge(s_dve, chain[0])

            V = nc.vector

            def rsqrt(y, x, t):
                yield V.tensor_scalar(t.bitcast(I32), x.bitcast(I32), 1, None, ALU.logical_shift_right)
                yield V.tensor_scalar(y.bitcast(I32), t.bitcast(I32), -1.0, RSQRT_GUESS, ALU.mult, ALU.add)
                for _ in range(NEWTON):
                    yield V.tensor_tensor(t, y, y, ALU.mult)
                    yield V.scalar_tensor_tensor(out=t, in0=t, scalar=-0.5, in1=x, op0=ALU.mult, op1=ALU.mult)
                    yield V.scalar_tensor_tensor(out=y, in0=t, scalar=1.5, in1=y, op0=ALU.add, op1=ALU.mult)

            def layernorm(first, last, between):
                for g in range(first, last):
                    dve.wait_ge(s_x[g], 16)
                    for n in range(g * BPG, (g + 1) * BPG):
                        ins = V.bn_stats(stats[:, n, :], x_sb[:, n, :])
                        if first > 0 and n < last * BPG - 1:
                            next(between, None)
                ns = slice(first * BPG, last * BPG)
                link(ins)
                for n in range(first * BPG, last * BPG):
                    ins = V.bn_aggr(mean_var[:, n, :], stats[:, n, :])
                link(ins)
                link(V.tensor_scalar(var[:, ns], mean_var[:, ns, 1], LN_EPS, None, ALU.add))
                for ins in rsqrt(rstd[:, ns], var[:, ns], halves[:, ns]):
                    n = settled(ins)
                    next(between, None)
                    dve.wait_ge(s_dve, n)
                for g in range(first, last):
                    for n in range(g * BPG, (g + 1) * BPG):
                        ins = V.tensor_scalar(xn[:, n, 0:D], x_sb[:, n, :], mean_var[:, n, 0:1], rstd[:, n:n + 1],
                                              ALU.subtract, ALU.mult)
                    ins.then_inc(s_xn, 1)

            def settled(ins):
                chain[0] += 1
                ins.then_inc(s_dve, 1)
                return chain[0]

            def centroids():
                dve.wait_ge(s_cent, 16)
                n = settled(V.tensor_tensor(cent_sq[:], cent[:], cent[:], ALU.mult))
                yield
                dve.wait_ge(s_dve, n)
                n = settled(V.tensor_reduce(cent_s[:, 0:1], cent_sq[:], AX.X, ALU.add))
                yield
                dve.wait_ge(s_dve, n)
                for ins in rsqrt(cent_s[:, 2:3], cent_s[:, 0:1], cent_s[:, 1:2]):
                    n = settled(ins)
                    yield
                    dve.wait_ge(s_dve, n)
                n = settled(V.tensor_scalar(cent_s[:, 3:4], cent_s[:, 2:3], MAX_NORM, 1.0, ALU.mult, ALU.min))
                yield
                dve.wait_ge(s_dve, n)
                V.tensor_scalar(cent_p[:], cent[:], cent_s[:, 3:4], None, ALU.mult).then_inc(s_cp, 1)
                yield
                yield
                yield
                dve.wait_ge(s_cpe, 1)
                n = settled(V.tensor_copy(cp_t[:], bank[7][:, 0:E]))
                yield
                dve.wait_ge(s_dve, n)
                V.tensor_tensor(cp_sq[:], cp_t[:], cp_t[:], ALU.mult).then_inc(s_cpt, 1)
                yield
                yield
                yield
                dve.wait_ge(s_cpe, 2)
                dve.wait_ge(s_b1t, 1)
                n = settled(V.tensor_scalar(c_n2[:], bank[7][:, E:2 * E], NORM_CAP, None, ALU.min))
                yield
                dve.wait_ge(s_dve, n)
                V.tensor_scalar(c_om[:], c_n2[:], -1.0, 1.0, ALU.mult, ALU.add)
                yield
                V.tensor_copy(b1[:].rearrange("p e c -> p (e c)"), bank[7][:, 2 * E:2 * E + E * FC]).then_inc(s_b1, 1)

            def queries(g):
                dve.wait_ge(s_sigq, g + 1)
                V.scalar_tensor_tensor(out=q_t[:, g, :], in0=bank[I_F_Q_BANKS[g][2]][:], scalar=QSCALE, in1=sig_q[:, g % 2],
                                       op0=ALU.mult, op1=ALU.mult).then_inc(s_q, 1)

            fill = centroids()
            layernorm(0, 1, fill)
            layernorm(1, G, fill)
            for _ in fill:
                pass
            queries(0)

            def tok(i):
                return r_tok[i][:].unsqueeze(2).to_broadcast([P, NB, E])

            def exp(a):
                return a[:].unsqueeze(1).to_broadcast([P, NB, E])

            def routing():
                dve.wait_ge(s_rp, G)
                V.tensor_copy(prod[:], bank[7][:, 0:NB * E].rearrange("p (n e) -> p n e", e=E))
                dve.wait_ge(s_xnorm, G)
                for ins in rsqrt(r_tok[1][:], xnorm[:], r_tok[2][:]):
                    n = settled(ins)
                    yield
                    dve.wait_ge(s_dve, n)
                n = settled(V.tensor_scalar(r_tok[2][:], r_tok[1][:], MAX_NORM, 1.0, ALU.mult, ALU.min))
                yield
                dve.wait_ge(s_dve, n)
                V.tensor_tensor(r_big[0][:], prod[:], tok(2), ALU.mult)
                n = settled(V.tensor_tensor(r_tok[3][:], xnorm[:], r_tok[2][:], ALU.mult))
                yield
                dve.wait_ge(s_dve, n)
                n = settled(V.tensor_tensor(r_tok[4][:], r_tok[3][:], r_tok[2][:], ALU.mult))
                yield
                dve.wait_ge(s_dve, n)
                n = settled(V.tensor_scalar(r_tok[5][:], r_tok[4][:], NORM_CAP, None, ALU.min))
                yield
                dve.wait_ge(s_dve, n)
                n = settled(V.scalar_tensor_tensor(out=r_big[1][:], in0=r_big[0][:], scalar=-2.0, in1=tok(5), op0=ALU.mult, op1=ALU.add))
                yield
                dve.wait_ge(s_dve, n)
                V.tensor_tensor(r_big[2][:], r_big[1][:], exp(c_n2), ALU.add)
                n = settled(V.tensor_scalar(r_tok[6][:], r_tok[5][:], -1.0, 1.0, ALU.mult, ALU.add))
                yield
                dve.wait_ge(s_dve, n)
                n = settled(V.tensor_tensor(r_big[3][:], tok(6), exp(c_om), ALU.mult))
                yield
                dve.wait_ge(s_dve, n)
                n = settled(V.tensor_scalar(r_big[4][:], r_big[3][:], BALL_EPS, None, ALU.add))
                yield
                dve.wait_ge(s_dve, n)
                V.tensor_scalar(r_big[1][:], r_big[2][:], 0.0, 2.0, ALU.max, ALU.mult)
                n = settled(V.reciprocal(r_big[5][:], r_big[4][:]))
                yield
                dve.wait_ge(s_dve, n)
                n = settled(V.tensor_tensor(r_big[6][:], r_big[1][:], r_big[5][:], ALU.mult))
                yield
                dve.wait_ge(s_dve, n)
                n = settled(V.tensor_scalar(r_big[0][:], r_big[6][:], 1.0, ARG_MIN, ALU.add, ALU.max))
                yield
                dve.wait_ge(s_dve, n)
                hot = (r_big[7], r_big[8])
                arg = r_big[0]
                for k in range(TOPK):
                    n = settled(V.tensor_reduce(m12[:, k, :], arg[:], AX.X, ALU.min))
                    yield
                    dve.wait_ge(s_dve, n)
                    n = settled(V.tensor_tensor(r_big[2][:], arg[:], m12[:, k, :].unsqueeze(2).to_broadcast([P, NB, E]), ALU.is_equal))
                    yield
                    dve.wait_ge(s_dve, n)
                    n = settled(V.scalar_tensor_tensor(out=r_big[3][:], in0=r_big[2][:], scalar=-float(E), in1=exp(iota_e8),
                                                op0=ALU.mult, op1=ALU.add))
                    yield
                    dve.wait_ge(s_dve, n)
                    n = settled(V.tensor_reduce(r_tok[7][:], r_big[3][:], AX.X, ALU.min))
                    yield
                    dve.wait_ge(s_dve, n)
                    n = settled(V.tensor_tensor(hot[k][:], exp(iota_e), tok(7), ALU.is_equal))
                    yield
                    dve.wait_ge(s_dve, n)
                    if k == 0:
                        n = settled(V.scalar_tensor_tensor(out=r_big[1][:], in0=hot[0][:], scalar=FAR, in1=arg[:], op0=ALU.mult, op1=ALU.add))
                        yield
                        dve.wait_ge(s_dve, n)
                        arg = r_big[1]
                V.tensor_tensor(r_big[9][:], hot[0][:], hot[1][:], ALU.add).then_inc(s_route, 1)
                sides = [weights(), places(hot)]
                for _ in range(8):
                    next(sides[0])
                    yield
                while sides:
                    for side in list(sides):
                        try:
                            next(side)
                            yield
                        except StopIteration:
                            sides.remove(side)

            def weights():
                n = settled(V.tensor_scalar(u_a[:], m12[:], 1.0, None, ALU.subtract))
                yield
                dve.wait_ge(s_dve, n)
                n = settled(V.scalar_tensor_tensor(out=u_b[:], in0=m12[:], scalar=1.0, in1=u_a[:], op0=ALU.add, op1=ALU.mult))
                yield
                dve.wait_ge(s_dve, n)
                for ins in rsqrt(u_a[:], u_b[:], u_c[:]):
                    n = settled(ins)
                    yield
                    dve.wait_ge(s_dve, n)
                n = settled(V.tensor_tensor(u_c[:], u_a[:], u_b[:], ALU.mult))
                yield
                dve.wait_ge(s_dve, n)
                n = settled(V.tensor_tensor(u_b[:], u_c[:], m12[:], ALU.add))
                yield
                dve.wait_ge(s_dve, n)
                n = settled(V.reciprocal(u_a[:, 1, :], u_b[:, 1, :]))
                yield
                dve.wait_ge(s_dve, n)
                n = settled(V.tensor_tensor(r_tok[0][:], u_b[:, 0, :], u_a[:, 1, :], ALU.mult))
                yield
                dve.wait_ge(s_dve, n)
                n = settled(V.tensor_scalar(r_tok[1][:], r_tok[0][:], 1.0, None, ALU.add))
                yield
                dve.wait_ge(s_dve, n)
                n = settled(V.reciprocal(weight[:, 0, :], r_tok[1][:]))
                yield
                dve.wait_ge(s_dve, n)
                n = settled(V.tensor_tensor(weight[:, 1, :], r_tok[0][:], weight[:, 0, :], ALU.mult))
                yield
                dve.wait_ge(s_dve, n)
            def places(hot):
                dve.wait_ge(s_rank, 1)
                rank = bank[5][:, 0:NB * E].rearrange("p (n e) -> p e n", e=E)
                total = bank[5][:, NB * E:2 * NB * E].rearrange("p (n e) -> p e n", e=E)
                n = settled(V.tensor_copy(tot[:], total))
                yield
                dve.wait_ge(s_dve, n)
                n = settled(V.tensor_tensor_scan(inc[:].rearrange("p e n -> p (e n)"), not_first[:].rearrange("p e n -> p (e n)"),
                                          tot[:].rearrange("p e n -> p (e n)"), 0.0, ALU.mult, ALU.add))
                yield
                dve.wait_ge(s_dve, n)
                V.tensor_tensor(exc[:], inc[:], tot[:], ALU.subtract)
                n = settled(V.tensor_scalar(cnt_i[:, 0, :], inc[:, :, NB - 1], float(P - 1), None, ALU.add))
                yield
                dve.wait_ge(s_dve, n)
                SH = P.bit_length() - 1
                n = settled(V.tensor_scalar(cnt_i[:, 1, :], cnt_i[:, 0, :], SH, SH, ALU.logical_shift_right, ALU.logical_shift_left))
                yield
                dve.wait_ge(s_dve, n)
                n = settled(V.tensor_copy(pad_f[:, 0, :], cnt_i[:, 1, :]))
                yield
                dve.wait_ge(s_dve, n)
                n = settled(V.tensor_tensor_scan(pad_f[:, 1, :], ones[:, 0:E], pad_f[:, 0, :], 0.0, ALU.mult, ALU.add))
                yield
                dve.wait_ge(s_dve, n)
                n = settled(V.tensor_tensor(pad_f[:, 2, :], pad_f[:, 1, :], pad_f[:, 0, :], ALU.subtract))
                yield
                dve.wait_ge(s_dve, n)
                n = settled(V.tensor_tensor(tot[:], exc[:], pad_f[:, 2, :].unsqueeze(2).to_broadcast([P, E, NB]), ALU.add))
                yield
                dve.wait_ge(s_dve, n)
                n = settled(V.tensor_tensor(inc[:], rank, tot[:], ALU.add))
                yield
                dve.wait_ge(s_dve, n)
                for k in range(TOPK):
                    n = settled(V.tensor_tensor(r_big[2 + k][:], hot[k][:], inc[:].rearrange("p e n -> p n e"), ALU.mult))
                yield
                for k in range(TOPK):
                    dve.wait_ge(s_dve, n - 1 + k)
                    V.tensor_reduce(pos_f[:, k, :], r_big[2 + k][:], AX.X, ALU.add).then_inc(s_dve, 1)
                chain[0] += TOPK
                n = chain[0]
                yield
                dve.wait_ge(s_dve, n)
                V.tensor_copy(pos[:], pos_f[:]).then_inc(s_pos, 1)
                V.tensor_tensor(own_f[:], pad_f[0:1, 1, :].unsqueeze(1).to_broadcast([1, TILES, E]),
                                tile_row[:].unsqueeze(2).to_broadcast([1, TILES, E]), ALU.is_le).then_inc(s_ended, 1)

            def scans(g, j):
                n = g * DK + j
                dve.wait_ge(s_vb, n + 1)
                if not isinstance(n, int) or n >= 4:
                    dve.wait_ge(*multiplied(n - 4))
                V.tensor_tensor_scan(state[:, j % 4].rearrange("p b t -> p (b t)"),
                                     gate[:, bass.ds(g * GB, GB), :].rearrange("p b t -> p (b t)"),
                                     pair[j % 2][:].rearrange("p b t -> p (b t)")[:, BANK - TP:BANK + TP], 0.0, ALU.mult, ALU.add).then_inc(s_scan, 1)

            def times_q(g, j):
                n = g * DK + j
                dve.wait_ge(s_scan, n + 1)
                if not isinstance(n, int) or n >= 2:
                    dve.wait_ge(s_red, n - 1)
                V.tensor_tensor(qstate[:, j % 2].rearrange("p (b t) -> p b t", b=GB), state[:, j % 4, :, 1:T + 1],
                                q_t[:, bass.ds(g, 1), :].rearrange("p o (b t) -> p (o b) t", b=GB),
                                ALU.mult).then_inc(s_qs, 1)

            def finish(g):
                done = RMS_STEPS * g
                dve.wait_ge(s_ms, g + 1)
                V.tensor_scalar(rms[:, 0, :], norm2[:], 1.0 / D, RMS_EPS, ALU.mult, ALU.add).then_inc(s_rms, 1)
                yield
                dve.wait_ge(s_rms, done + 1)
                for k, ins in enumerate(rsqrt(rms[:, 1, :], rms[:, 0, :], rms[:, 2, :])):
                    ins.then_inc(s_rms, 1)
                    yield
                    dve.wait_ge(s_rms, done + k + 2)
                dve.wait_ge(s_att, g + 1)
                for j in range(BPG):
                    if j > 0:
                        yield
                    n = bass.ds(g * BPG + j, 1)
                    ins = V.scalar_tensor_tensor(out=acc[:, n, :].rearrange("p o d -> p (o d)"), in0=bank[7][:, j * D:(j + 1) * D],
                                                 scalar=rms[:, 1, j:j + 1], in1=x_sb[:, n, :].rearrange("p o d -> p (o d)"),
                                                 op0=ALU.mult, op1=ALU.add)
                    if isinstance(g, int) and g == G - 1 and j == BPG // 2 - 1:
                        ins.then_inc(s_half, 1)
                ins.then_inc(s_acc, 1)

            def add_up(g):
                dve.wait_ge(s_red, (g + 1) * DK)
                dve.wait_ge(s_qv, g + 1)
                V.tensor_tensor(o_t[:], bank[4][:], q_v[:], ALU.add).then_inc(s_ot, 1)

            def attention(g, first, last, between, start, each):
                for j in range(DK):
                    if j + 1 < DK:
                        scans(g, j + 1)
                    elif not last:
                        if first:
                            dve.wait_ge(s_gate, G)
                        scans(g + 1, 0)
                    if j == 0 and not first and not last:
                        add_up(g - 1)
                    if j >= start:
                        for _ in range(each):
                            next(between, None)
                    if not first or j not in ON_POOL:
                        times_q(g, j)
                    if first and j % 3 == 0 and QUERIES_AT <= j < QUERIES_AT + 3 * (G - 1):
                        queries((j - QUERIES_AT) // 3 + 1)
                    if j >= start:
                        for _ in range(each):
                            next(between, None)
                    if j == 1:
                        if not first:
                            dve.wait_ge(s_ot, g)
                        dve.wait_ge(s_qsum, g + 1)
                        V.tensor_tensor(q_v[:].rearrange("p (b t) -> p b t", b=GB), bank[5][:].rearrange("p (b t) -> p b t", b=GB),
                                        v_t[:, bass.ds(g * GB, GB), 2:T + 2], ALU.mult).then_inc(s_qv, 1)
                for _ in between:
                    pass

            dve.wait_ge(s_gate, 1)
            scans(0, 0)
            attention(0, True, False, routing(), 0, ROUTING_EACH)
            dve.wait_ge(*multiplied(ON_POOL[-1]))
            with dve.Fori(1, G - 1) as g:
                attention(g, False, False, finish(g - 1), 4, 1)

            def take_weights(t, u, e):
                V.tensor_copy(w1_now[u % 2][:], w1[:, bass.ds(e, 1), :].rearrange("p o f -> p (o f)")).then_inc(s_w1, 1)

            def take_places(t, u):
                V.tensor_copy(place[u][:], xs[u][:, D:D + 1].bitcast(U32)).then_inc(s_place, 1)

            def bias1(t, u, e):
                dve.wait_ge(s_l1, t + 1)
                V.tensor_tensor(hb[u % 2][:].rearrange("p (c t) -> p c t", c=FC), bank[2 + u % 2][:].rearrange("p (c t) -> p c t", c=FC),
                                b1[:, bass.ds(e, 1), :].rearrange("p o c -> p (o c)").unsqueeze(2).to_broadcast([P, FC, P]),
                                ALU.add).then_inc(s_hb, 1)

            def bias2(t, u, e):
                dve.wait_ge(s_place, t + 1)
                V.tensor_copy(place_y[u][:], place[u][:])
                dve.wait_ge(s_l2, t + 1)
                V.tensor_tensor(yb[u][:], bank[u % 2][:, 0:D], b2[:, bass.ds(e, 1), :].rearrange("p o f -> p (o f)"), ALU.add).then_inc(s_yb, 1)

            def experts(t, n):
                regs = [dve.alloc_register(f"expert_{k}_{next(serial)}") for k in range(n)]
                dve.load(regs, own[0:1, bass.ds(t, n)])
                return [dve.snap(r, min_val=0, max_val=E - 1) for r in regs]

            dve.wait_ge(s_wexp, 48)
            dve.wait_ge(s_own, 1)
            ex = experts(0, 3)
            take_weights(0, 0, ex[0])
            add_up(G - 2)
            take_weights(1, 1, ex[1])
            for t in range(3):
                dve.wait_ge(s_xs[t], 16)
                take_places(t, t)
            bias1(0, 0, ex[0])
            take_weights(2, 2, ex[2])
            bias1(1, 1, ex[1])

            last_finish = finish(G - 2)

            def between(i):
                if isinstance(i, int):
                    next(last_finish, None)

            def steps(i):
                ex = experts(RING * i, RING + LAG)
                for u in range(RING):
                    s = RING * i + LAG + u
                    a, b, c = (LAG + u) % RING, (LAG + u - 1) % RING, u
                    dve.wait_ge(s_l1, s - 1)
                    between(i)
                    take_weights(s, a, ex[u + LAG])
                    between(i)
                    dve.wait_ge(s_hg, s - 2)
                    bias1(s - 1, b, ex[u + LAG - 1])
                    dve.wait_ge(s_xs[a], 16 * (i + (LAG + u) // RING + 1))
                    if not isinstance(s, int) or s > 3:
                        dve.wait_ge(s_yb, s - 3)
                    between(i)
                    take_places(s, a)
                    if not isinstance(i, int):
                        dve.wait_ge(s_ys[c], 16 * i)
                    bias2(s - 3, c, ex[u])
                    between(i)

            steps(0)
            with dve.Fori(1, ROUNDS) as i:
                steps(i)
            ex = experts(TILES - 3, 3)
            dve.wait_ge(s_hg, TILES - 2)
            bias1(TILES - 1, (TILES - 1) % RING, ex[2])
            for t in range(TILES - 3, TILES):
                dve.wait_ge(s_ys[t % RING], 16 * (t // RING))
                bias2(t, t % RING, ex[t - TILES + 3])
            dve.wait_ge(s_again, 2)
            attention(G - 1, False, True, iter(()), DK, 0)
            add_up(G - 1)
            dve.wait_ge(s_fin, G)
            for _ in finish(G - 1):
                pass


_INS = ["L0_attn_hidden_states", "L0_attn_Wq", "L0_attn_Wf", "L0_attn_Wi", "L0_attn_g_weight", "L0_attn_Wo",
        "L0_ffn_centroids", "L0_ffn_Wp", "L0_ffn_bp", "L0_ffn_W1", "L0_ffn_b1", "L0_ffn_W2", "L0_ffn_b2"]


def kernel(**inputs):
    import numpy as _np
    import concourse.bacc as _bacc
    from concourse import mybir as _mybir
    from concourse.bass_utils import run_bass_kernel_spmd as _run

    nc = _bacc.Bacc("TRN2", target_bir_lowering=False, num_devices=1)
    arrays, args = {}, []
    for name in _INS:
        a = _np.ascontiguousarray(inputs[name])
        arrays[f"in_{name}_dram"] = a
        args.append(nc.dram_tensor(f"in_{name}_dram", a.shape, _mybir.dt.from_np(a.dtype), kind="ExternalInput").ap())
    shape = inputs["L0_attn_hidden_states"].shape
    args.append(nc.dram_tensor("out_0_dram", shape, _mybir.dt.float32, kind="ExternalOutput").ap())
    gla_and_routed_experts(nc, *args)
    r = _run(nc, [arrays], core_ids=[0])
    return r.results[0]["out_0_dram"]
```
